# Optimizing a Trainium2 kernel written in Bass

```python
import numpy as np
import jax
import jax.numpy as jnp

def _softmax(x, axis=-1):
    return jax.nn.softmax(x, axis=axis)

def _gelu(x):
    return jax.nn.gelu(x, approximate=True)

def _silu(x):
    return jax.nn.silu(x)

def _sigmoid(x):
    return jax.nn.sigmoid(x)

def _layernorm(x, axis=-1, eps=1e-05):
    m = jnp.mean(x, axis=axis, keepdims=True)
    v = jnp.var(x, axis=axis, keepdims=True)
    return (x - m) / jnp.sqrt(v + eps)

def _scatter_add(tgt, idx, src, axis=0):
    return tgt.at[idx].add(src)

def _segment_sum(src, seg, n):
    return jax.ops.segment_sum(src, seg, n)
kernel_name = 'mk_gnn_ffn_d1_gnn_r8_6375b1'

def setup_inputs(seed: int=0):
    np.random.seed(seed)
    _w = jnp.asarray

    def _rec_inputs():
        import jax
        import jax.numpy as jnp
        _gk = jax.random.key(seed)
        x = 7.22e-05 + 1 * jax.random.normal(jax.random.fold_in(_gk, 1), (1250, 512), jnp.float32)
        _s = jax.random.randint(jax.random.fold_in(_gk, 2), (10000,), 0, 1250, jnp.int32)
        _d = jax.random.randint(jax.random.fold_in(_gk, 3), (10000,), 0, 1250, jnp.int32)
        _loop = jnp.arange(1250, dtype=jnp.int32)
        src = jnp.concatenate([_s, _d, _loop])
        dst = jnp.concatenate([_d, _s, _loop])
        _o = jnp.argsort(dst, stable=True)
        src = src[_o]
        dst = dst[_o]
        edge_weight = jax.random.uniform(jax.random.fold_in(_gk, 12), (21250,), jnp.float32, 0.0, 0.999994)
        return (x, src, dst, edge_weight)
    x, src, dst, edge_weight = _rec_inputs()

    def _L0_gnn_setup():
        import jax, jax.numpy as jnp
        import numpy as np
        N = 2048
        D = 512
        NNZ = 20480
        NUM_ITERS = 10
        key = jax.random.key(seed)
        k1, k2, k3, k4 = jax.random.split(key, 4)
        x = jax.random.normal(k1, (N, D), dtype=jnp.float32)
        edge_val = jax.random.uniform(k2, (NNZ,), dtype=jnp.float32)
        edge_row = jnp.sort(jax.random.randint(k3, (NNZ,), 0, N, dtype=jnp.int32))
        edge_col = jax.random.randint(k4, (NNZ,), 0, N, dtype=jnp.int32)
        alpha = jnp.zeros((1,), dtype=jnp.float32)
        beta = jnp.zeros((1,), dtype=jnp.float32)
        sigma = jnp.ones((1,), dtype=jnp.float32)
        return {'x': x, 'alpha': alpha, 'beta': beta, 'sigma': sigma, 'edge_val': edge_val, 'edge_row': edge_row, 'edge_col': edge_col, 'num_iters': NUM_ITERS}
    _L0_gnn_all = _L0_gnn_setup()
    _L0_gnn_in = {k: v for k, v in _L0_gnn_all.items() if k in ('alpha', 'beta', 'sigma')}
    del _L0_gnn_all

    def _L0_ffn_setup():
        import jax, jax.numpy as jnp
        import numpy as np
        B, T, I, H, S = (64, 128, 512, 512, 4)

        def _lstm_activate(gates, c):
            i, f, g, o = jnp.split(gates, 4, axis=-1)
            c_new = jax.nn.sigmoid(f) * c + jax.nn.sigmoid(i) * jnp.tanh(g)
            h_new = jax.nn.sigmoid(o) * jnp.tanh(c_new)
            return (h_new, c_new)
        key = jax.random.key(seed)
        ks = jax.random.split(key, 7)
        sc_i = 1.0 / np.sqrt(I)
        sc_h = 1.0 / np.sqrt(H)
        x = jax.random.normal(ks[0], (B, T, I), jnp.float32)
        W_ih = jax.random.normal(ks[1], (S, 4 * H, I), jnp.float32) * sc_i
        W_hh = jax.random.normal(ks[2], (S, 4 * H, H), jnp.float32) * sc_h
        b_ih = jax.random.normal(ks[3], (S, 4 * H), jnp.float32) * sc_h
        b_hh = jax.random.normal(ks[4], (S, 4 * H), jnp.float32) * sc_h
        W_sel = jax.random.normal(ks[5], (S, 2 * H + I), jnp.float32) * sc_h
        b_sel = jax.random.normal(ks[6], (S,), jnp.float32) * sc_h
        return {'x': x, 'W_ih': W_ih, 'W_hh': W_hh, 'b_ih': b_ih, 'b_hh': b_hh, 'W_sel': W_sel, 'b_sel': b_sel}
    _L0_ffn_all = _L0_ffn_setup()
    _L0_ffn_in = {k: v for k, v in _L0_ffn_all.items() if k in ('W_ih', 'W_hh', 'b_ih', 'b_hh', 'W_sel', 'b_sel')}
    del _L0_ffn_all
    return {'x': x, 'src': src, 'dst': dst, 'edge_weight': edge_weight, 'L0_gnn_alpha': _L0_gnn_in['alpha'], 'L0_gnn_beta': _L0_gnn_in['beta'], 'L0_gnn_sigma': _L0_gnn_in['sigma'], 'L0_ffn_W_ih': _L0_ffn_in['W_ih'], 'L0_ffn_W_hh': _L0_ffn_in['W_hh'], 'L0_ffn_b_ih': _L0_ffn_in['b_ih'], 'L0_ffn_b_hh': _L0_ffn_in['b_hh'], 'L0_ffn_W_sel': _L0_ffn_in['W_sel'], 'L0_ffn_b_sel': _L0_ffn_in['b_sel']}

def reference(x, src, dst, edge_weight, L0_gnn_alpha, L0_gnn_beta, L0_gnn_sigma, L0_ffn_W_ih, L0_ffn_W_hh, L0_ffn_b_ih, L0_ffn_b_hh, L0_ffn_W_sel, L0_ffn_b_sel):
    import jax
    import jax.numpy as jnp

    def _L0_gnn_ref(x, alpha, beta, sigma, edge_val, edge_row, edge_col, num_iters):
        import jax, jax.numpy as jnp
        import numpy as np
        N = 2048
        D = 512
        NNZ = 20480
        NUM_ITERS = 10
        n = x.shape[0]
        xn = x * jax.lax.rsqrt(jnp.maximum(jnp.sum(x * x, axis=1, keepdims=True), 1e-12))
        sim_e = jnp.sum(xn[edge_row] * xn[edge_col], axis=-1)
        sim_e = jnp.where(edge_row == edge_col, 0.0, sim_e)
        s = jnp.exp(sigma[0])
        sigma_sq = 2.0 * s * s
        sim_e = jnp.exp(sim_e / (2.0 * sigma_sq))
        sup = edge_val * sim_e
        normalize = jax.ops.segment_sum(sup, edge_row, num_segments=n)
        a = jnp.exp(alpha[0])
        b = jnp.exp(beta[0])
        denom = b + normalize[:, None] * a + a

        def step(out, _):
            Ax = jax.ops.segment_sum(sup[:, None] * out[edge_col], edge_row, num_segments=n)
            out = (x * b + (Ax + out) * a) / denom
            return (out, None)
        out, _ = jax.lax.scan(step, x, None, length=num_iters)
        return out

    def _L0_ffn_ref(x, W_ih, W_hh, b_ih, b_hh, W_sel, b_sel):
        import jax, jax.numpy as jnp
        import numpy as np
        B, T, I, H, S = (64, 128, 512, 512, 4)

        def _lstm_activate(gates, c):
            i, f, g, o = jnp.split(gates, 4, axis=-1)
            c_new = jax.nn.sigmoid(f) * c + jax.nn.sigmoid(i) * jnp.tanh(g)
            h_new = jax.nn.sigmoid(o) * jnp.tanh(c_new)
            return (h_new, c_new)
        Bx, Tx, Ix = x.shape
        Sx, fourH, _ = W_ih.shape
        Hx = fourH // 4
        c0 = jnp.zeros((Bx, Hx), x.dtype)
        g0 = x[:, 0] @ W_ih[0].T + b_ih[0] + b_hh[0]
        h, c = _lstm_activate(g0, c0)

        def step(carry, x_t):
            h, c = carry
            sel_in = jnp.concatenate([h, c, x_t], axis=-1)
            logits = sel_in @ W_sel.T + b_sel
            onehot = jax.nn.one_hot(jnp.argmax(logits, axis=-1), Sx, dtype=x_t.dtype)
            g_all = jnp.einsum('bi,sgi->bsg', x_t, W_ih) + jnp.einsum('bh,sgh->bsg', h, W_hh) + b_ih + b_hh
            g = jnp.einsum('bsg,bs->bg', g_all, onehot)
            h2, c2 = _lstm_activate(g, c)
            return ((h2, c2), h2)
        xs = jnp.swapaxes(x[:, 1:], 0, 1)
        (_, _), hs = jax.lax.scan(step, (h, c), xs)
        outputs = jnp.concatenate([h[:, None], jnp.swapaxes(hs, 0, 1)], axis=1)
        return outputs
    x = x + _L0_gnn_ref(_layernorm(x, axis=-1), L0_gnn_alpha, L0_gnn_beta, L0_gnn_sigma, edge_weight, src, dst, 10)
    x = x + _L0_ffn_ref(_layernorm(x, axis=-1)[None], L0_ffn_W_ih, L0_ffn_W_hh, L0_ffn_b_ih, L0_ffn_b_hh, L0_ffn_W_sel, L0_ffn_b_sel)[0]
    return x

_drawn_inputs = setup_inputs


def setup_inputs(seed=0):
    import zlib

    import numpy as np

    out = dict(_drawn_inputs(seed))
    spreads = {}
    factors = {}
    for name, (base, spread) in spreads.items():
        noise = np.random.default_rng([zlib.crc32(name.encode()), seed]).standard_normal(out[name].shape)
        drawn = base * np.exp(spread * noise) if base else spread * noise
        out[name] = jnp.asarray(drawn.astype(out[name].dtype))
    for name, factor in factors.items():
        out[name] = (out[name] * factor).astype(out[name].dtype)
    return out
```

```python
import concourse.bass as bass
from concourse import mybir
from contextlib import ExitStack


def gnn_then_selected_lstm(
    nc: bass.Bass,
    x: bass.AP,
    src_main: bass.AP,
    src_tail: bass.AP,
    dst_main: bass.AP,
    dst_tail: bass.AP,
    ew_main: bass.AP,
    ew_tail: bass.AP,
    scalars: bass.AP,
    w_ih: bass.AP,
    w_hh: bass.AP,
    b_ih: bass.AP,
    b_hh: bass.AP,
    w_sel_state: bass.AP,
    w_sel_x: bass.AP,
    out: bass.AP,
):
    f32, f16, i32, u32 = mybir.dt.float32, mybir.dt.float16, mybir.dt.int32, mybir.dt.uint32
    ALU, ACT, AX = mybir.AluOpType, mybir.ActivationFunctionType, mybir.AxisListType

    P = 128
    N, D = x.shape
    RT = -(-N // P)
    NP = RT * P
    LAST = N - (RT - 1) * P
    KC = D // P
    S = w_sel_x.shape[2]
    G = 4
    SUB = D // P
    EC = src_main.shape[1]
    ET = src_tail.shape[0]
    ECP = -(-(EC + 1) // 2) * 2
    NN = NP * NP
    CW = NN // P + 1
    ITERS = 10
    COLS = [(c, min(512, NP - c)) for c in range(0, NP, 512)]
    TB = 250
    TBN = N // TB
    TG = 25
    NBLK = N // TG
    EPS = 1e-5
    WARM = 5
    A, B = 11, 13
    GATE_SCALE = float(2 ** (A + B + 1))
    W_COLS = S * KC * 4 * D

    adj = [nc.dram_tensor(f"adjacency_{b}", (P * CW,), f32, kind="Internal").ap() for b in range(2)]
    gx_dram = nc.dram_tensor("gate_inputs", (S, P, N, G * SUB), f32, kind="Internal").ap()
    lx_dram = nc.dram_tensor("logit_inputs", (NP, S), f32, kind="Internal").ap()
    pick_dram = nc.dram_tensor("guessed_sets", (NP,), i32, kind="Internal").ap()
    x1_dram = nc.dram_tensor("x1_rows", (NP, D), f32, kind="Internal").ap()

    ctx = ExitStack()
    with ctx:
        def sb(name, shape, dt, where=ctx):
            return where.enter_context(nc.sbuf_tensor(name, shape, dt))

        def sem(name):
            return ctx.enter_context(nc.semaphore(name))

        ident = sb("ident", [P, P], f32)
        ones = sb("ones", [P, P], f32)
        xT = sb("xT", [P, KC, NP], f32)
        scal = sb("scal", [1, 3 + S], f32)
        scal_b = sb("scal_b", [P, 3 + S], f32)
        ab = sb("ab", [P, 4], f32)
        stats = sb("stats", [P, RT, 6], f32)
        mv = sb("mv", [P, RT, 2], f32)
        rstd = sb("rstd", [P, RT], f32)
        square = sb("square", [P, RT], f32)
        root = sb("root", [P, RT], f32)
        newton = sb("newton", [P, RT], f32)
        ramp = sb("ramp", [P, S], f32)
        biases = sb("biases", [P, S * G * SUB], f32)
        bias2 = sb("bias2", [P, S * G * SUB], f32)
        wselx = sb("wselx", [P, KC, S], f32)
        wsel = sb("wsel", [P, S, 2 * SUB], f32)
        lx_t = sb("lx_t", [P, RT, S], f32)
        lx_w = sb("lx_w", [P, RT, S], f32)
        lx_m = sb("lx_m", [P, RT], f32)
        pick_t = sb("pick_t", [P, RT], i32)
        with ExitStack() as graph:
            X = sb("X", [P, RT, D], f32, graph)
            O0 = sb("O0", [P, RT, D], f32, graph)
            O1 = sb("O1", [P, RT, D], f32, graph)
            Adj = sb("Adj", [P, RT, NP], f32, graph)
            Adj1 = sb("Adj1", [P, CW], f32, graph)
            sim = sb("sim", [P, 2, NP], f32, graph)
            not_ident = sb("not_ident", [P, P], f32, graph)
            below = sb("below", [P, P], f32, graph)
            src_i = sb("src_i", [P, ECP], i32, graph)
            dst_i = sb("dst_i", [P, ECP], i32, graph)
            src_f = sb("src_f", [P, ECP], f32, graph)
            dst_f = sb("dst_f", [P, ECP], f32, graph)
            ew = sb("ew", [P, ECP], f32, graph)
            key = sb("key", [P, ECP], f32, graph)
            to_dump = sb("to_dump", [P, ECP], f32, graph)
            dump_i = sb("dump_i", [P, 1], i32, graph)
            dump_f = sb("dump_f", [P, 1], f32, graph)
            kdiag = sb("kdiag", [P, 2, P], f32, graph)
            same = sb("same", [P, 2, P], f32, graph)
            junk = sb("junk", [P, 2, P], f32, graph)
            earlier = sb("earlier", [P, 2], f32, graph)
            shift = sb("shift", [P, 2], f32, graph)
            total = sb("total", [P, 2, 1], f32, graph)
            where_ = sb("where_", [P, 2, 1], u32, graph)
            sumsq = sb("sumsq", [P, RT], f32, graph)
            den = sb("den", [P, RT], f32, graph)
            adn = sb("adn", [P, RT], f32, graph)
            bdn = sb("bdn", [P, RT], f32, graph)
        XB = Adj1[:, 0:RT * D].rearrange("p (t d) -> p t d", t=RT)

        WH = sb("WH", [P, S * KC, 2, 4, D], f16)
        with ExitStack() as project:
            wst = sb("wst", [P, 2, 2, D], f32, project)
            wih = sb("wih", [P, G, KC, D], f32, project)
            gstage = sb("gstage", [P, TB, G * SUB], f32, project)
        gateT = sb("gateT", [P, G * SUB, 33], f32)
        gates = sb("gates", [P, G * SUB], f32)
        acts = sb("acts", [P, G * SUB + SUB], f32)
        cprod = sb("cprod", [P, 2 * SUB], f32)
        osig = sb("osig", [P, SUB], f32)
        tanc = sb("tanc", [P, SUB], f32)
        hfull = sb("hfull", [P, SUB], f32)
        hparts = sb("hparts", [P, SUB, 17], f16)
        lprod = sb("lprod", [P, S, 2 * SUB + 1], f32)
        lpart = sb("lpart", [P, S], f32)
        lmax = sb("lmax", [1, 1], f32)
        lmark = sb("lmark", [1, S], f32)
        pick = sb("pick", [1, 1], i32)
        hist = xT
        gblk = sb("gblk", [P, 2, S, TG, G * SUB], f32)
        lx_row = sb("lx_row", [1, NP, S], f32)
        pick_row = sb("pick_row", [1, NP], i32)
        x1_t = sb("x1_t", [P, 2, D], f32)
        out_t = sb("out_t", [P, 2, D], f32)

        ps = ctx.enter_context(nc.psum_tensor("ps", [P, 8, 512], f32))
        gate_ps = ps[:, 0, :]
        logit_ps = ps[0:1, 1, 0:S]
        seal_ps = ps[0:1, 2, 0:1]

        x_in = sem("x_in")
        square_ready = sem("square_ready")
        root_ready = sem("root_ready")
        edges_in = sem("edges_in")
        adj_zeroed = sem("adj_zeroed")
        places_free = [sem(f"places_free{b}") for b in range(2)]
        small_in = sem("small_in")
        zero_set = sem("zero_set")
        consts = sem("consts")
        masks = sem("masks")
        v = sem("v")
        a = sem("a")
        scal_mm = sem("scal_mm")
        ab_ready = sem("ab_ready")
        xn_ready = sem("xn_ready")
        trans_mm = sem("trans_mm")
        trans_out = sem("trans_out")
        edge_ready = sem("edge_ready")
        kd_ready = [sem(f"kd_ready{b}") for b in range(2)]
        kr_ready = [sem(f"kr_ready{b}") for b in range(2)]
        same_ready = [sem(f"same_ready{b}") for b in range(2)]
        earlier_ready = [sem(f"earlier_ready{b}") for b in range(2)]
        shift_ready = [sem(f"shift_ready{b}") for b in range(2)]
        total_mm = [sem(f"total_mm{b}") for b in range(2)]
        edge_out = [sem(f"edge_out{b}") for b in range(2)]
        places_ready = [sem(f"places_ready{b}") for b in range(2)]
        prop_ready = sem("prop_ready")
        scattered = [sem(f"scattered{b}") for b in range(2)]
        adj_in = sem("adj_in")
        adj_sum = sem("adj_sum")
        sim_mm = sem("sim_mm")
        sim_masked = sem("sim_masked")
        sim_exp = sem("sim_exp")
        adj_ready = sem("adj_ready")
        deg_mm = sem("deg_mm")
        prop_mm = sem("prop_mm")
        o_part = sem("o_part")
        o_ready = sem("o_ready")
        x1_ready = sem("x1_ready")
        x1_out = sem("x1_out")
        y_ready = sem("y_ready")
        lx_mm = sem("lx_mm")
        lx_ready = sem("lx_ready")
        lx_out = sem("lx_out")
        graph_free = sem("graph_free")
        wih_in = [sem(f"wih_in{g}") for g in range(G)]
        proj_mm = sem("proj_mm")
        proj_out = sem("proj_out")
        gx_stored = sem("gx_stored")
        whh_in = [sem(f"whh_in{b}") for b in range(2)]
        whh_scaled = [sem(f"whh_scaled{b}") for b in range(2)]
        whh_high = [sem(f"whh_high{b}") for b in range(2)]
        whh_low = [sem(f"whh_low{b}") for b in range(2)]
        rows_in = sem("rows_in")
        gblk_in = [sem(f"gblk_in{b}") for b in range(2)]
        gblk_used = [sem(f"gblk_used{b}") for b in range(2)]
        lx0_set = sem("lx0_set")
        lx_next = sem("lx_next")
        hist_free = sem("hist_free")
        h_ready = sem("h_ready")
        lpart_ready = sem("lpart_ready")
        logits_mm = sem("logits_mm")
        lmax_ready = sem("lmax_ready")
        lmark_ready = sem("lmark_ready")
        pick_ready = sem("pick_ready")
        scatter_seen = sem("scatter_seen")
        pick_seen = sem("pick_seen")
        gates_mm = sem("gates_mm")
        turned = sem("turned")
        gx_set = sem("gx_set")
        gates_ready = sem("gates_ready")
        acts_ready = sem("acts_ready")
        cprod_ready = sem("cprod_ready")
        osig_ready = sem("osig_ready")
        c_ready = sem("c_ready")
        tanc_ready = sem("tanc_ready")
        h_full = sem("h_full")
        lprod_c = sem("lprod_c")
        lprod_h = sem("lprod_h")
        x1_back = [sem(f"x1_back{b}") for b in range(2)]
        out_mm = sem("out_mm")
        out_sum = sem("out_sum")
        out_done = [sem(f"out_done{b}") for b in range(2)]

        EIT = ECP // 2
        NCH = len(COLS)
        TQ = [(q, min(4, RT - q)) for q in range(0, RT, 4)]
        NTQ = KC * len(TQ)

        block = ctx.enter_context(nc.Block())

        @block.sync
        def _(sp):
            sp.wait_ge(zero_set, 1)
            sp.dma_start(X[:, 0:RT - 1, :], x[0:(RT - 1) * P, :].rearrange("(t p) d -> p t d", p=P)).then_inc(x_in, 16)
            sp.dma_start(X[0:LAST, RT - 1, :], x[(RT - 1) * P:N, :]).then_inc(x_in, 16)
            sp.wait_ge(zero_set, 2)
            for b in range(2):
                sp.dma_start(adj[b].rearrange("(p n) -> p n", p=P), Adj1[:, :]).then_inc(adj_zeroed, 16)
            for b in range(2):
                sp.wait_ge(scattered[b], 16 * EIT)
            sp.dma_start(Adj[:, :, :], adj[0][0:NN].rearrange("(t p n) -> p t n", p=P, n=NP)).then_inc(adj_in, 16)
            sp.dma_start(Adj1[:, 0:RT * NP].rearrange("p (t n) -> p t n", t=RT),
                         adj[1][0:NN].rearrange("(t p n) -> p t n", p=P, n=NP)).then_inc(adj_in, 16)
            sp.wait_ge(x1_ready, 1)
            sp.dma_start(x1_dram.rearrange("(t p) d -> p t d", p=P), X[:, :, :]).then_inc(x1_out, 16)
            sp.wait_ge(lx_ready, 1)
            sp.dma_start(lx_dram.rearrange("(t p) s -> p t s", p=P), lx_t[:, :, :]).then_inc(lx_out, 16)
            sp.dma_start(pick_dram.rearrange("(t p) -> p t", p=P), pick_t[:, :], allow_slow_non_contiguous=True).then_inc(lx_out, 16)
            sp.wait_ge(x1_out, 16)
            sp.wait_ge(graph_free, 1)
            for g in range(G):
                sp.dma_start(wih[:, g, :, :].rearrange("p k n -> p (k n)"), w_ih[:, 0, g, :]).then_inc(wih_in[g], 16)

            def store(s, tb):
                sp.wait_ge(proj_out, sp.snap((s * TBN + tb + 1) * (G * SUB) + 8))
                sp.dma_start(gx_dram[bass.ds(s, 1), :, bass.ds(tb * TB, TB), :].rearrange("a p t c -> p (a t c)"),
                             gstage[:, :, :].rearrange("p t c -> p (t c)")).then_inc(gx_stored, 16)

            with sp.Fori(0, S - 1) as s:
                with sp.Fori(0, TBN - 1) as tb:
                    store(s, tb)
                for g in range(G):
                    sp.wait_ge(proj_mm, sp.snap((s * TBN + TBN - 1) * (G * SUB) + (g + 1) * SUB))
                    sp.dma_start(wih[:, g, :, :].rearrange("p k n -> p (k n)"),
                                 w_ih[:, bass.ds(s + 1, 1), g, :].rearrange("p a n -> p (a n)")).then_inc(wih_in[g], 16)
                store(s, TBN - 1)
            with sp.Fori(0, TBN) as tb:
                store(S - 1, tb)
            sp.wait_ge(gx_stored, 16 * (S * TBN + 1))
            sp.wait_ge(lx_out, 32)
            for b in range(2):
                sp.wait_ge(whh_low[b], S * KC + 1)
            sp.dma_start(lx_row[0:1, :, :], lx_dram.rearrange("(a t) s -> a t s", a=1)).then_inc(rows_in, 16)
            sp.dma_start(pick_row[0:1, :], pick_dram.rearrange("(a t) -> a t", a=1)).then_inc(rows_in, 16)

            def load_block(t0, b):
                sp.dma_start(gblk[:, b, :, :, :].rearrange("p s t c -> p s (t c)"),
                             gx_dram[:, :, bass.ds(t0, TG), :].rearrange("s p t c -> p s (t c)")).then_inc(gblk_in[b], 16)

            for b in range(2):
                load_block(b * TG, b)
            with sp.Fori(1, NBLK // 2) as i:
                n = sp.snap(i)
                for b in range(2):
                    sp.wait_ge(gblk_used[b], n)
                    load_block(i * (2 * TG) + b * TG, b)
            for t in range(RT):
                b = t % 2
                if t >= 2:
                    sp.wait_ge(out_sum, SUB * (t - 1))
                sp.dma_start(x1_t[:, b, :], x1_dram[t * P:(t + 1) * P, :]).then_inc(x1_back[b], 16)
            for b in range(2):
                sp.wait_ge(out_done[b], 16 * (RT // 2))

        @block.gpsimd
        def _(pool):
            pool.wait_ge(consts, 1)
            pool.affine_select(out=below[:, :], in_=ones[:, :], compare_op=ALU.is_gt, fill=0.0, base=0,
                               pattern=[[-1, P]], channel_multiplier=1).then_inc(masks, 1)
            pool.affine_select(out=not_ident[:, :], in_=ones[:, :], compare_op=ALU.not_equal, fill=0.0, base=0,
                               pattern=[[-1, P]], channel_multiplier=1).then_inc(masks, 1)
            pool.wait_ge(consts, 2)
            pool.affine_select(out=ident[:, :], in_=ident[:, :], compare_op=ALU.not_equal, fill=1.0, base=0,
                               pattern=[[-1, P]], channel_multiplier=1).then_inc(masks, 1)
            pool.iota(dump_i[:, :], pattern=[[0, 1]], base=NN, channel_multiplier=1).then_inc(masks, 1)
            last_word = pool.alloc_register("last_word")
            pool.reg_mov(last_word, P * CW - 1)
            pool.wait_ge(adj_zeroed, 32)
            for b in range(2):
                pool.sem_inc(places_free[b], 1)
            with pool.Fori(0, EIT) as i:
                n = pool.snap(i + 1)
                n16 = pool.snap(i * 16 + 16)
                for b in range(2):
                    pool.wait_ge(places_ready[b], n)
                    pool.wait_ge(edge_out[b], n)
                    pool.sem_inc(scatter_seen, 1)
                    pool.indirect_dma_start(
                        out=adj[b].rearrange("(n a) -> n a", a=1),
                        out_offset=bass.IndirectOffsetOnAxis(ap=where_[:, b, :], axis=0),
                        in_=total[:, b, :], in_offset=None, compute_op=ALU.add,
                        bounds_check=last_word, oob_is_err=True).then_inc(scattered[b], 16)
                for b in range(2):
                    pool.wait_ge(scattered[b], n16)
                    pool.sem_inc(places_free[b], 1)
            for b in range(2):
                pool.sem_inc(whh_low[b], 1)
            with pool.Fori(0, S * KC) as i:
                n = pool.snap(i + 1)
                for b in range(2):
                    pool.wait_ge(whh_high[b], n)
                    pool.tensor_tensor(WH[:, bass.ds(i, 1), 1, 2 * b:2 * b + 2, :].rearrange("p a j n -> p (a j n)"),
                                       wst[:, b, :, :].rearrange("p j n -> p (j n)"),
                                       WH[:, bass.ds(i, 1), 0, 2 * b:2 * b + 2, :].rearrange("p a j n -> p (a j n)"),
                                       ALU.subtract).then_inc(whh_low[b], 1)
            pool.wait_ge(rows_in, 32)
            pool.wait_ge(lx_ready, 2)
            pool.tensor_copy(lprod[0:1, :, 2 * SUB], lx_row[0:1, 0, :]).then_inc(lx0_set, 1)
            with pool.Fori(0, N) as t:
                n = pool.snap(t + 1)
                n2 = pool.snap(t * 2 + 2)
                pool.wait_ge(lpart_ready, n)
                pool.tensor_copy(lprod[0:1, :, 2 * SUB:2 * SUB + 1].rearrange("a s c -> a (s c)"),
                                 lx_row[0:1, bass.ds(t + 1, 1), :].rearrange("a t s -> a (t s)")).then_inc(lx_next, 1)
                pool.wait_ge(h_full, n2)
                pool.tensor_copy(hist[:, :, bass.ds(t, 1)].rearrange("p s t -> p (s t)"), hfull[:, :]).then_inc(hist_free, 1)

        @block.scalar
        def _(act):
            chain = [0]

            def link(ins):
                chain[0] += 1
                ins.then_inc(a, 1)
                act.wait_ge(a, chain[0])

            act.dma_start(scal[:, :], scalars).then_inc(small_in, 16)
            act.dma_start(biases[:, :], b_ih).then_inc(small_in, 16)
            act.dma_start(bias2[:, :], b_hh).then_inc(small_in, 16)
            act.dma_start(wselx[:, :, :], w_sel_x).then_inc(small_in, 16)
            act.dma_start(wsel[:, :, :], w_sel_state).then_inc(small_in, 16)
            act.wait_ge(edge_ready, 1)
            for tile, main, tail in ((src_i, src_main, src_tail), (dst_i, dst_main, dst_tail), (ew, ew_main, ew_tail)):
                act.dma_start(tile[:, 0:EC], main).then_inc(edges_in, 16)
                act.dma_start(tile[0:ET, EC:EC + 1], tail).then_inc(edges_in, 16)
            act.wait_ge(scal_mm, 2)
            act.activation(ab[:, 0:2], scal_b[:, 0:2], ACT.Exp).then_inc(ab_ready, 1)
            act.activation(ab[:, 2:3], scal_b[:, 2:3], ACT.Exp, scale=-2.0).then_inc(ab_ready, 1)

            def take_root(n):
                act.wait_ge(square_ready, n)
                act.activation(root[:, :], square[:, :], ACT.Sqrt).then_inc(root_ready, 1)

            take_root(1)
            take_root(2)

            def evacuate_transposes(first):
                for k in range(KC):
                    for q, (r0, m) in enumerate(TQ):
                        i = first + k * len(TQ) + q
                        act.wait_ge(trans_mm, i + 1)
                        act.activation(xT[:, k, r0 * P:(r0 + m) * P], ps[:, i % 8, 0:m * P], ACT.Copy).then_inc(trans_out, 1)

            evacuate_transposes(0)
            act.wait_ge(ab_ready, 3)
            for r in range(RT):
                for c, (c0, m) in enumerate(COLS):
                    act.wait_ge(sim_mm, NCH * r + c + 1)
                    if c0 <= r * P < c0 + m:
                        act.wait_ge(sim_masked, r + 1)
                    if r >= 2:
                        act.wait_ge(adj_ready, r - 1)
                    act.activation(sim[:, r % 2, c0:c0 + m], ps[:, 2 + 3 * (r % 2) + c, 0:m], ACT.Exp,
                                   scale=ab[:, 3:4]).then_inc(sim_exp, 1)
            take_root(3)
            evacuate_transposes(NTQ)
            act.wait_ge(x1_out, 16)
            act.wait_ge(graph_free, 1)
            w_v = w_hh.rearrange("p (c b n) -> p c b n", c=S * KC, b=2)

            with act.Fori(0, S * KC) as i:
                n = act.snap(i + 1)
                n2 = act.snap(i * 2 + 2)
                n16 = act.snap(i * 16 + 16)
                for b in range(2):
                    act.wait_ge(whh_low[b], n)
                    act.dma_start(wst[:, b, :, :].rearrange("p j n -> p (j n)"),
                                  w_v[:, bass.ds(i, 1), b, :].rearrange("p a n -> p (a n)")).then_inc(whh_in[b], 16)
                for b in range(2):
                    act.wait_ge(whh_in[b], n16)
                    act.activation(wst[:, b, :, 0:3 * P], wst[:, b, :, 0:3 * P], ACT.Copy, scale=float(2 ** (A - 1))).then_inc(whh_scaled[b], 1)
                    act.activation(wst[:, b, :, 3 * P:D], wst[:, b, :, 3 * P:D], ACT.Copy, scale=float(2 ** A)).then_inc(whh_scaled[b], 1)
                for b in range(2):
                    act.wait_ge(whh_scaled[b], n2)
                    act.activation(WH[:, bass.ds(i, 1), 0, 2 * b:2 * b + 2, :].rearrange("p a j n -> p (a j n)"),
                                   wst[:, b, :, :].rearrange("p j n -> p (j n)"), ACT.Copy).then_inc(whh_high[b], 1)
            act.activation(root[:, :], square[:, :], ACT.Tanh)
            with act.Fori(0, NBLK // 2) as i:
                nb = act.snap(i * 16 + 16)
                for b in range(2):
                    act.wait_ge(gblk_in[b], nb)
                    with act.Fori(0, TG) as tl:
                        n = act.snap(i * (2 * TG) + tl + (b * TG + 1))
                        act.wait_ge(pick_ready, n)
                        act.sem_inc(pick_seen, 1)
                        r = act.value_load(pick[0:1, 0:1], min_val=1, max_val=S)
                        act.activation(gateT[:, :, 32:33].rearrange("p c a -> p (c a)"),
                                       gblk[:, b, bass.ds(r - 1, 1), bass.ds(tl, 1), :].rearrange("p s t c -> p (s t c)"),
                                       ACT.Copy).then_inc(gx_set, 1)
                        act.wait_ge(gates_ready, n)
                        act.activation(acts[:, 0:G * SUB], gates[:, :], ACT.Tanh, scale=1.0 / GATE_SCALE).then_inc(acts_ready, 1)
                        act.wait_ge(c_ready, n)
                        act.activation(tanc[:, :], acts[:, G * SUB:G * SUB + SUB], ACT.Tanh, scale=0.5).then_inc(tanc_ready, 1)
                    act.sem_inc(gblk_used[b], 1)
            for t in range(RT):
                b = t % 2
                rows = P if t < RT - 1 else LAST
                act.wait_ge(out_sum, SUB * (t + 1))
                act.dma_start(out[t * P:t * P + rows, :], out_t[0:rows, b, :]).then_inc(out_done[b], 16)

        @block.vector
        def _(dve):
            chain = [0]

            def link(ins):
                chain[0] += 1
                ins.then_inc(v, 1)
                dve.wait_ge(v, chain[0])

            dve.memset(X[:, RT - 1, :], 0.0).then_inc(zero_set, 1)
            dve.memset(Adj1[:, :], 0.0).then_inc(zero_set, 1)
            dve.memset(ones[:, :], 1.0).then_inc(consts, 1)
            dve.memset(ident[:, :], 0.0).then_inc(consts, 1)
            dve.memset(src_i[:, :], 0)
            dve.memset(dst_i[:, :], 0)
            dve.memset(ew[:, :], 0.0).then_inc(edge_ready, 1)
            for s in range(S):
                link(dve.memset(ramp[:, s:s + 1], float(S - s)))

            dve.wait_ge(scal_mm, 1)
            dve.tensor_copy(scal_b[:, :], ps[:, 7, 0:3 + S]).then_inc(scal_mm, 1)
            dve.wait_ge(ab_ready, 2)
            dve.tensor_scalar(ab[:, 3:4], ab[:, 2:3], 0.25, None, ALU.mult).then_inc(ab_ready, 1)

            roots = [0]

            def inverse_root(to):
                roots[0] += 1
                dve.sem_inc(square_ready, 1)
                dve.wait_ge(root_ready, roots[0])
                link(dve.reciprocal(to[:, :], root[:, :]))
                link(dve.tensor_tensor(newton[:, :], to[:, :], to[:, :], ALU.mult))
                link(dve.tensor_tensor(newton[:, :], newton[:, :], square[:, :], ALU.mult))
                link(dve.tensor_scalar(newton[:, :], newton[:, :], -0.5, 1.5, ALU.mult, ALU.add))
                link(dve.tensor_tensor(to[:, :], to[:, :], newton[:, :], ALU.mult))

            def layernorm_stats():
                for r in range(RT):
                    dve.bn_stats(stats[:, r, :], X[:, r, :]).then_inc(v, 1)
                    chain[0] += 1
                dve.wait_ge(v, chain[0])
                for r in range(RT):
                    dve.bn_aggr(mv[:, r, :], stats[:, r, :]).then_inc(v, 1)
                    chain[0] += 1
                dve.wait_ge(v, chain[0])
                link(dve.tensor_scalar(square[:, :], mv[:, :, 1], EPS, None, ALU.add))
                inverse_root(rstd)

            dve.wait_ge(x_in, 32)
            layernorm_stats()
            for r in range(RT):
                link(dve.tensor_scalar(O0[:, r, :], X[:, r, :], mv[:, r, 0:1], rstd[:, r:r + 1], ALU.subtract, ALU.mult))
                link(dve.scalar_tensor_tensor(out=O1[:, r, :], in0=O0[:, r, :], scalar=1.0, in1=O0[:, r, :],
                                              op0=ALU.mult, op1=ALU.mult, accum_out=sumsq[:, r:r + 1]))
            link(dve.tensor_scalar(square[:, :], sumsq[:, :], 1e-12, None, ALU.max))
            inverse_root(sumsq)
            for r in range(RT):
                dve.tensor_scalar(O1[:, r, :], O0[:, r, :], sumsq[:, r:r + 1], None, ALU.mult).then_inc(xn_ready, 1)

            dve.wait_ge(masks, 4)
            link(dve.tensor_copy(dump_f[:, :], dump_i[:, :]))
            dve.wait_ge(edges_in, 16 * 6)
            link(dve.tensor_copy(src_f[:, :], src_i[:, :]))
            link(dve.tensor_copy(dst_f[:, :], dst_i[:, :]))
            for c in range(EC, ECP):
                link(dve.tensor_copy(key[:, c:c + 1], dump_f[:, :]))
            link(dve.scalar_tensor_tensor(out=key[:, 0:EC], in0=dst_f[:, 0:EC], scalar=float(NP), in1=src_f[:, 0:EC],
                                          op0=ALU.mult, op1=ALU.add))
            link(dve.scalar_tensor_tensor(out=key[0:ET, EC:EC + 1], in0=dst_f[0:ET, EC:EC + 1], scalar=float(NP),
                                          in1=src_f[0:ET, EC:EC + 1], op0=ALU.mult, op1=ALU.add))
            link(dve.tensor_scalar(to_dump[:, :], key[:, :], dump_f[:, 0:1], -1.0, ALU.subtract, ALU.mult))
            with dve.Fori(0, EIT) as i:
                n = dve.snap(i + 1)
                kcol = [key[:, bass.ds(i * 2 + b, 1)] for b in range(2)]
                dcol = [to_dump[:, bass.ds(i * 2 + b, 1)] for b in range(2)]
                for b in range(2):
                    dve.tensor_scalar(kdiag[:, b, :], ident[:, :], kcol[b], None, ALU.mult).then_inc(kd_ready[b], 1)
                for b in range(2):
                    dve.wait_ge(kr_ready[b], n)
                    dve.tensor_scalar(same[:, b, :], ps[:, 2 * b, 0:P], kcol[b], None, ALU.is_equal).then_inc(same_ready[b], 1)
                    dve.scalar_tensor_tensor(out=junk[:, b, :], in0=ps[:, 2 * b, 0:P], scalar=kcol[b], in1=below[:, :],
                                             op0=ALU.is_equal, op1=ALU.mult, accum_out=earlier[:, b:b + 1]).then_inc(earlier_ready[b], 1)
                for b in range(2):
                    dve.wait_ge(earlier_ready[b], n)
                    dve.scalar_tensor_tensor(out=shift[:, b:b + 1], in0=earlier[:, b:b + 1], scalar=1.0, in1=dcol[b],
                                             op0=ALU.min, op1=ALU.mult).then_inc(shift_ready[b], 1)
                for b in range(2):
                    dve.wait_ge(shift_ready[b], n)
                    dve.wait_ge(places_free[b], n)
                    dve.tensor_tensor(where_[:, b, :], shift[:, b:b + 1], kcol[b], ALU.add).then_inc(places_ready[b], 1)
                    dve.wait_ge(total_mm[b], n)
                    dve.tensor_copy(total[:, b, :], ps[:, 2 * b + 1, 0:1]).then_inc(edge_out[b], 1)
            dve.wait_ge(adj_in, 32)
            for r in range(RT):
                dve.tensor_tensor(Adj[:, r, :], Adj[:, r, :], Adj1[:, r * NP:(r + 1) * NP], ALU.add).then_inc(adj_sum, 1)
            for r in range(RT):
                c = r // 4
                q = r * P - COLS[c][0]
                dve.wait_ge(sim_mm, NCH * r + c + 1)
                blk = ps[:, 2 + 3 * (r % 2) + c, q:q + P]
                dve.tensor_tensor(blk, blk, not_ident[:, :], ALU.mult).then_inc(sim_masked, 1)
                dve.wait_ge(adj_sum, r + 1)
                dve.wait_ge(sim_exp, NCH * (r + 1))
                dve.tensor_tensor(Adj[:, r, :], Adj[:, r, :], sim[:, r % 2, :], ALU.mult).then_inc(adj_ready, 1)
            dve.wait_ge(deg_mm, 1)
            link(dve.tensor_scalar(den[:, :], ps[:, 0, 0:RT], ab[:, 0:1], ab[:, 1:2], ALU.mult, ALU.add))
            link(dve.tensor_scalar(den[:, :], den[:, :], ab[:, 0:1], None, ALU.add))
            link(dve.reciprocal(den[:, :], den[:, :]))
            link(dve.tensor_scalar(adn[:, :], den[:, :], ab[:, 0:1], None, ALU.mult))
            link(dve.tensor_scalar(bdn[:, :], den[:, :], ab[:, 1:2], None, ALU.mult))
            for r in range(RT):
                link(dve.tensor_scalar(XB[:, r, :], O0[:, r, :], bdn[:, r:r + 1], None, ALU.mult))
            dve.sem_inc(prop_ready, 1)
            with dve.Fori(0, ITERS // 2) as i:
                for half, (old, new) in enumerate(((O0, O1), (O1, O0))):
                    for r in range(RT):
                        dve.scalar_tensor_tensor(out=new[:, r, :], in0=old[:, r, :], scalar=adn[:, r:r + 1], in1=XB[:, r, :],
                                                 op0=ALU.mult, op1=ALU.add).then_inc(o_part, 1)
                    for r in range(RT):
                        n = dve.snap(i * (2 * RT) + (half * RT + r + 1))
                        dve.wait_ge(o_part, n)
                        dve.wait_ge(prop_mm, n)
                        dve.scalar_tensor_tensor(out=new[:, r, :], in0=ps[:, r % 8, :], scalar=adn[:, r:r + 1], in1=new[:, r, :],
                                                 op0=ALU.mult, op1=ALU.add).then_inc(o_ready, 1)
                    dve.wait_ge(o_ready, n)
            dve.wait_ge(o_ready, ITERS * RT)
            for r in range(RT):
                link(dve.tensor_tensor(X[:, r, :], X[:, r, :], O0[:, r, :], ALU.add))
            dve.sem_inc(x1_ready, 1)
            layernorm_stats()
            for r in range(RT):
                dve.tensor_scalar(O1[:, r, :], X[:, r, :], mv[:, r, 0:1], rstd[:, r:r + 1], ALU.subtract, ALU.mult).then_inc(y_ready, 1)
            dve.wait_ge(small_in, 16 * 5)
            dve.wait_ge(lx_mm, 1)
            bsel = scal_b[:, 3:3 + S].rearrange("p (a s) -> p a s", a=1).broadcast_to([P, RT, S])
            link(dve.tensor_tensor(lx_t[:, :, :], ps[:, 0, 0:RT * S].rearrange("p (t s) -> p t s", s=S), bsel, ALU.add))
            link(dve.memset(lx_t[0:1, 0, :], 0.0))
            link(dve.memset(lx_t[0:1, 0, 0:1], 1.0))
            link(dve.tensor_reduce(lx_m[:, :], lx_t[:, :, :], AX.X, ALU.max))
            link(dve.tensor_tensor(lx_w[:, :, :], lx_t[:, :, :], lx_m[:, :].rearrange("p (t a) -> p t a", a=1).broadcast_to([P, RT, S]), ALU.is_ge))
            link(dve.tensor_tensor(lx_w[:, :, :], lx_w[:, :, :], ramp[:, :].rearrange("p (a s) -> p a s", a=1).broadcast_to([P, RT, S]), ALU.mult))
            dve.tensor_reduce(pick_t[:, :], lx_w[:, :, :], AX.X, ALU.max).then_inc(lx_ready, 1)
            link(dve.tensor_tensor(biases[:, :], biases[:, :], bias2[:, :], ALU.add))
            bv = biases[:, :].rearrange("p (s g c) -> p s g c", s=S, g=G)
            link(dve.tensor_scalar(bv[:, :, 0:3, :], bv[:, :, 0:3, :], GATE_SCALE / 2, None, ALU.mult))
            link(dve.tensor_scalar(bv[:, :, 3:4, :], bv[:, :, 3:4, :], GATE_SCALE, None, ALU.mult))
            link(dve.tensor_scalar(wsel[:, :, 0:SUB], wsel[:, :, 0:SUB], 0.5, None, ALU.mult))
            link(dve.tensor_scalar(wsel[:, :, SUB:2 * SUB], wsel[:, :, SUB:2 * SUB], float(2.0 ** -(B + 1)), None, ALU.mult))
            dve.wait_ge(graph_free, 1)
            dve.wait_ge(x1_out, 16)
            dve.sem_inc(proj_out, 8)
            dve.sem_inc(gx_stored, 16)
            with dve.Fori(0, S) as s:
                with dve.Fori(0, TBN) as tb:
                    stored = dve.snap((s * TBN + tb) * 16 + 16)
                    for c in range(G * SUB):
                        if c == 0:
                            dve.wait_ge(gx_stored, stored)
                        dve.wait_ge(proj_mm, dve.snap((s * TBN + tb) * (G * SUB) + (c + 1)))
                        dve.tensor_scalar(gstage[:, :, c], ps[:, c % 8, 0:TB], GATE_SCALE if c // SUB == 3 else GATE_SCALE / 2,
                                          biases[:, bass.ds(s * (G * SUB) + c, 1)], ALU.mult, ALU.add).then_inc(proj_out, 1)
            for b in range(2):
                dve.wait_ge(whh_low[b], S * KC + 1)
            dve.wait_ge(gx_stored, 16 * (S * TBN + 1))
            dve.wait_ge(proj_mm, S * TBN * G * SUB)
            dve.wait_ge(proj_out, S * TBN * G * SUB + 8)
            link(dve.memset(gateT[:, :, :], 0.0))
            link(dve.memset(gate_ps, 0.0))
            link(dve.memset(acts[:, G * SUB:G * SUB + SUB], 0.0))
            link(dve.memset(lprod[:, :, :], 0.0))
            dve.sem_inc(lx_ready, 1)
            dve.memset(hparts[:, :, :], 0.0).then_inc(h_ready, 1)
            dve.sem_inc(hist_free, 1)
            dve.wait_ge(lx0_set, 1)
            dve.tensor_reduce(lpart[:, :], lprod[:, :, :], AX.X, ALU.add).then_inc(lpart_ready, 1)

            def choose(n):
                dve.wait_ge(logits_mm, n)
                dve.tensor_reduce(lmax[:, :], logit_ps, AX.X, ALU.max).then_inc(lmax_ready, 1)
                dve.wait_ge(lmax_ready, n)
                dve.scalar_tensor_tensor(out=lmark[:, :], in0=logit_ps, scalar=lmax[:, 0:1], in1=ramp[0:1, :],
                                         op0=ALU.is_ge, op1=ALU.mult).then_inc(lmark_ready, 1)
                dve.wait_ge(lmark_ready, n)
                dve.tensor_reduce(pick[:, :], lmark[:, :], AX.X, ALU.max).then_inc(pick_ready, 1)

            def cell(n, n2):
                dve.wait_ge(gates_mm, n)
                dve.transpose(gateT[:, :, 0:32], gate_ps.rearrange("p (c q) -> p c q", q=32)).then_inc(turned, 1)
                dve.wait_ge(turned, n)
                dve.wait_ge(gx_set, n)
                dve.tensor_reduce(gates[:, :], gateT[:, :, 0:33:16], AX.X, ALU.add).then_inc(gates_ready, 1)
                dve.wait_ge(acts_ready, n)
                dve.scalar_tensor_tensor(out=cprod[:, :], in0=acts[:, 0:2 * SUB], scalar=1.0, in1=acts[:, 3 * SUB:5 * SUB],
                                         op0=ALU.add, op1=ALU.mult).then_inc(cprod_ready, 1)
                dve.tensor_scalar(osig[:, :], acts[:, 2 * SUB:3 * SUB], 1.0, float(2 ** B), ALU.add, ALU.mult).then_inc(osig_ready, 1)
                dve.wait_ge(cprod_ready, n)
                dve.scalar_tensor_tensor(out=acts[:, 4 * SUB:5 * SUB], in0=cprod[:, SUB:2 * SUB], scalar=0.5, in1=cprod[:, 0:SUB],
                                         op0=ALU.mult, op1=ALU.add).then_inc(c_ready, 1)
                dve.wait_ge(osig_ready, n)
                dve.wait_ge(lx_next, n)
                dve.wait_ge(hist_free, n)
                dve.wait_ge(c_ready, n)
                dve.tensor_tensor(lprod[:, :, 0:SUB], acts[:, 4 * SUB:5 * SUB].rearrange("p (a c) -> p a c", a=1).broadcast_to([P, S, SUB]),
                                  wsel[:, :, 0:SUB], ALU.mult).then_inc(lprod_c, 1)
                dve.wait_ge(tanc_ready, n)
                dve.tensor_tensor(hfull[:, :], osig[:, :], tanc[:, :], ALU.mult).then_inc(h_full, 1)
                dve.tensor_tensor(hparts[:, :, 0], osig[:, :], tanc[:, :], ALU.mult).then_inc(h_full, 1)
                dve.wait_ge(h_full, n2)
                dve.tensor_tensor(hparts[:, :, 16], hfull[:, :], hparts[:, :, 0], ALU.subtract).then_inc(h_ready, 1)

            def logit_parts(n):
                dve.wait_ge(lprod_c, n)
                dve.tensor_tensor(lprod[:, :, SUB:2 * SUB], hfull[:, :].rearrange("p (a c) -> p a c", a=1).broadcast_to([P, S, SUB]),
                                  wsel[:, :, SUB:2 * SUB], ALU.mult).then_inc(lprod_h, 1)
                dve.wait_ge(lprod_h, n)
                dve.tensor_reduce(lpart[:, :], lprod[:, :, :], AX.X, ALU.add).then_inc(lpart_ready, 1)

            choose(1)
            with dve.Fori(0, N - 1) as t:
                n = dve.snap(t + 1)
                n2 = dve.snap(t * 2 + 2)
                after = dve.snap(t + 2)
                cell(n, n2)
                logit_parts(n)
                choose(after)
            cell(N, 2 * N)
            for t in range(RT):
                b = t % 2
                rows = P if t < RT - 1 else LAST
                if t >= 2:
                    dve.wait_ge(out_done[b], 16 * (t // 2))
                dve.wait_ge(x1_back[b], 16 * (t // 2 + 1))
                dve.wait_ge(out_mm, t + 1)
                x1_v = x1_t[0:rows, b, :].rearrange("p (j s q) -> p s j q", j=4, s=SUB)
                out_v = out_t[0:rows, b, :].rearrange("p (j s q) -> p s j q", j=4, s=SUB)
                for s in range(SUB):
                    dve.scalar_tensor_tensor(out=out_v[:, s, :, :],
                                             in0=ps[0:rows, 2 + b, s * P:(s + 1) * P].rearrange("p (j q) -> p j q", j=4),
                                             scalar=float(2.0 ** -(B + 1)), in1=x1_v[:, s, :, :],
                                             op0=ALU.mult, op1=ALU.add).then_inc(out_sum, 1)

        @block.tensor
        def _(pe):
            pe.wait_ge(consts, 1)
            pe.wait_ge(small_in, 16 * 5)
            nc.tensor.matmul(ps[:, 7, 0:3 + S], ones[0:1, :], scal[0:1, :], start=True, stop=True).then_inc(scal_mm, 1)
            pe.wait_ge(masks, 4)
            pe.wait_ge(scal_mm, 2)

            def transposes(src, first, ready, want):
                for k in range(KC):
                    for q, (r0, m) in enumerate(TQ):
                        i = first + k * len(TQ) + q
                        if i >= 8:
                            pe.wait_ge(trans_out, i - 7)
                        for r in range(r0, r0 + m):
                            if k == 0:
                                pe.wait_ge(ready, r + 1)
                            last = nc.tensor.transpose(ps[:, i % 8, (r - r0) * P:(r - r0 + 1) * P],
                                                       src[:, r, k * P:(k + 1) * P], ident[:, :])
                        last.then_inc(trans_mm, 1)

            transposes(O1, 0, xn_ready, 0)
            pe.wait_ge(trans_out, NTQ)
            with pe.Fori(0, EIT) as i:
                n = pe.snap(i + 1)
                for b in range(2):
                    pe.wait_ge(kd_ready[b], n)
                    nc.tensor.matmul(ps[:, 2 * b, 0:P], ones[:, :], kdiag[:, b, :], start=True, stop=True).then_inc(kr_ready[b], 1)
                for b in range(2):
                    pe.wait_ge(same_ready[b], n)
                    nc.tensor.matmul(ps[:, 2 * b + 1, 0:1], same[:, b, :], ew[:, bass.ds(i * 2 + b, 1)],
                                     start=True, stop=True).then_inc(total_mm[b], 1)
            pe.wait_ge(edge_out[0], EIT)
            pe.wait_ge(edge_out[1], EIT)
            for r in range(RT):
                for c, (c0, m) in enumerate(COLS):
                    if r >= 2:
                        pe.wait_ge(sim_exp, NCH * (r - 2) + c + 1)
                    for k in range(KC):
                        last = nc.tensor.matmul(ps[:, 2 + 3 * (r % 2) + c, 0:m], xT[:, k, r * P:(r + 1) * P],
                                                xT[:, k, c0:c0 + m], start=(k == 0), stop=(k == KC - 1))
                    last.then_inc(sim_mm, 1)
            pe.wait_ge(adj_ready, RT)
            for r in range(RT):
                for c in range(RT):
                    last = nc.tensor.matmul(ps[:, 0, r:r + 1], Adj[:, c, r * P:(r + 1) * P], ones[:, 0:1],
                                            start=(c == 0), stop=(c == RT - 1))
            last.then_inc(deg_mm, 1)
            pe.wait_ge(prop_ready, 1)
            with pe.Fori(0, ITERS // 2) as i:
                for half, old in enumerate((O0, O1)):
                    if half == 1:
                        pe.wait_ge(o_ready, pe.snap(i * (2 * RT) + RT))
                    for r in range(RT):
                        if r >= 8:
                            pe.wait_ge(o_ready, pe.snap(i * (2 * RT) + (half * RT + r - 7)))
                        for c in range(RT):
                            last = nc.tensor.matmul(ps[:, r % 8, :], Adj[:, c, r * P:(r + 1) * P], old[:, c, :],
                                                    start=(c == 0), stop=(c == RT - 1))
                        last.then_inc(prop_mm, 1)
                pe.wait_ge(o_ready, pe.snap(i * (2 * RT) + 2 * RT))
            transposes(O1, NTQ, y_ready, 0)
            pe.wait_ge(trans_out, 2 * NTQ)
            pe.sem_inc(graph_free, 1)
            for t in range(RT):
                for k in range(KC):
                    last = nc.tensor.matmul(ps[:, 0, t * S:(t + 1) * S], xT[:, k, t * P:(t + 1) * P], wselx[:, k, :],
                                            start=(k == 0), stop=(k == KC - 1))
            last.then_inc(lx_mm, 1)
            pe.wait_ge(lx_ready, 1)
            with pe.Fori(0, S) as s:
                n16 = pe.snap(s * 16 + 16)
                with pe.Fori(0, TBN) as tb:
                    for g in range(G):
                        pe.wait_ge(wih_in[g], n16)
                        for u in range(SUB):
                            c = g * SUB + u
                            done = pe.snap((s * TBN + tb) * (G * SUB) + (c + 1))
                            pe.wait_ge(proj_out, done)
                            for k in range(KC):
                                last = nc.tensor.matmul(ps[:, c % 8, 0:TB], wih[:, g, k, u * P:(u + 1) * P],
                                                        xT[:, k, bass.ds(tb * TB, TB)], start=(k == 0), stop=(k == KC - 1))
                            last.then_inc(proj_mm, 1)
            for b in range(2):
                pe.wait_ge(whh_low[b], S * KC + 1)

            def products(s, n, first):
                if first:
                    pe.wait_ge(h_ready, n)
                for k in range(KC):
                    for part in range(2):
                        if first and k == 1 and part == 0:
                            pe.wait_ge(lpart_ready, n)
                            nc.tensor.matmul(logit_ps, ones[:, 0:1], lpart[:, :], start=True, stop=True).then_inc(logits_mm, 1)
                        for j in range(4):
                            nc.tensor.matmul(gate_ps[32 * j:32 * j + 17, :], hparts[:, k, :], WH[:, s * KC + k, part, j, :],
                                             start=(k == 0 and part == 0), stop=(k == KC - 1 and part == 1),
                                             tile_position=(0, 32 * j))

            def products_of(chosen, n, first):
                with pe.If_lt(chosen, 3):
                    with pe.If_lt(chosen, 2):
                        products(3, n, first)
                    with pe.Else():
                        products(2, n, first)
                with pe.Else():
                    with pe.If_lt(chosen, 4):
                        products(1, n, first)
                    with pe.Else():
                        products(0, n, first)

            guess = pe.alloc_register("guess")
            chosen = pe.alloc_register("chosen")
            pe.wait_ge(rows_in, 32)
            pe.sem_inc(pick_seen, 1)
            with pe.Fori(0, N) as t:
                n = pe.snap(t + 1)
                pe.reg_load(guess, pick_row[0:1, bass.ds(t, 1)])
                products_of(guess, n, True)
                pe.wait_ge(pick_ready, n)
                pe.sem_inc(pick_seen, 1)
                pe.reg_load(chosen, pick[0:1, 0:1])
                with pe.If_ne(chosen, guess):
                    products_of(chosen, n, False)
                nc.tensor.matmul(seal_ps, hparts[:, 0, 0:1], hparts[:, 0, 0:1], start=True, stop=True).then_inc(gates_mm, 1)
                for _ in range(WARM):
                    nc.tensor.matmul(ps[:, 2, :], WH[:, 0, 0, 0, 0:P], WH[:, 0, 0, 0, :], start=True, stop=True)
            pe.wait_ge(hist_free, N + 1)
            for t in range(RT):
                rows = P if t < RT - 1 else LAST
                if t >= 2:
                    pe.wait_ge(out_sum, SUB * (t - 1))
                for s in range(SUB):
                    last = nc.tensor.transpose(ps[0:rows, 2 + t % 2, s * P:(s + 1) * P], hist[:, s, t * P:t * P + rows], ident[:, :])
                last.then_inc(out_mm, 1)


def kernel(**inputs):
    import numpy as np
    import concourse.bacc as bacc
    from concourse import mybir as mb
    from concourse.bass_utils import run_bass_kernel_spmd

    get = {k: np.asarray(val) for k, val in inputs.items()}
    P, D, S = 128, get["x"].shape[1], get["L0_ffn_W_ih"].shape[0]
    edges = get["src"].shape[0]
    main = edges // P * P
    order = [0, 1, 3, 2]

    def cut(a):
        return a[:main].reshape(P, main // P), a[main:].reshape(edges - main, 1)

    def by_unit(a):
        a = a.reshape(S, 4, 4, 4, 32)[::-1, order]
        return a.transpose(2, 4, 0, 1, 3).reshape(P, S * 16)

    whh = get["L0_ffn_W_hh"].reshape(S, 4, 4, P, 4, 4, 32)[:, order]
    whh = whh.transpose(4, 6, 0, 5, 2, 1, 3).reshape(P, S * 4 * 4 * D)
    wih = get["L0_ffn_W_ih"].reshape(S, 4, 4, 4, 32, 4, P)[::-1, order]
    wih = wih.transpose(6, 0, 1, 5, 3, 2, 4).reshape(P, S, 4, 4 * D)
    wsel = get["L0_ffn_W_sel"]
    wsel_h = wsel[:, 0:D].reshape(S, 4, 4, 32).transpose(1, 3, 0, 2).reshape(P, S, 4)
    wsel_c = wsel[:, D:2 * D].reshape(S, 4, 4, 32).transpose(1, 3, 0, 2).reshape(P, S, 4)
    src_main, src_tail = cut(get["src"])
    dst_main, dst_tail = cut(get["dst"])
    ew_main, ew_tail = cut(get["edge_weight"])
    arrays = {
        "x": get["x"],
        "src_main": src_main, "src_tail": src_tail,
        "dst_main": dst_main, "dst_tail": dst_tail,
        "ew_main": ew_main, "ew_tail": ew_tail,
        "scalars": np.concatenate([get["L0_gnn_alpha"], get["L0_gnn_beta"], get["L0_gnn_sigma"], get["L0_ffn_b_sel"]]).reshape(1, 3 + S),
        "w_ih": wih, "w_hh": whh,
        "b_ih": by_unit(get["L0_ffn_b_ih"]), "b_hh": by_unit(get["L0_ffn_b_hh"]),
        "w_sel_state": np.concatenate([wsel_c, wsel_h], axis=2),
        "w_sel_x": wsel[:, 2 * D:3 * D].reshape(S, 4, P).transpose(2, 1, 0),
    }
    nc = bacc.Bacc("TRN2", target_bir_lowering=False, num_devices=1)
    given, args = {}, []
    for name, a in arrays.items():
        a = np.ascontiguousarray(a)
        given[f"in_{name}"] = a
        args.append(nc.dram_tensor(f"in_{name}", a.shape, mb.dt.from_np(a.dtype), kind="ExternalInput").ap())
    out = nc.dram_tensor("out_rows", get["x"].shape, mb.dt.from_np(get["x"].dtype), kind="ExternalOutput").ap()
    gnn_then_selected_lstm(nc, *args, out)
    r = run_bass_kernel_spmd(nc, [given], core_ids=[0])
    return r.results[0]["out_rows"]
```

```python
import concourse.bass as bass
from concourse import mybir
from contextlib import ExitStack


def gnn_then_selected_lstm(
    nc: bass.Bass,
    x: bass.AP,
    src_main: bass.AP,
    src_tail: bass.AP,
    dst_main: bass.AP,
    dst_tail: bass.AP,
    ew_main: bass.AP,
    ew_tail: bass.AP,
    scalars: bass.AP,
    w_ih: bass.AP,
    w_hh: bass.AP,
    b_ih: bass.AP,
    b_hh: bass.AP,
    w_sel_state: bass.AP,
    w_sel_x: bass.AP,
    out: bass.AP,
):
    f32, f16, i32, u32 = mybir.dt.float32, mybir.dt.float16, mybir.dt.int32, mybir.dt.uint32
    ALU, ACT, AX = mybir.AluOpType, mybir.ActivationFunctionType, mybir.AxisListType

    P = 128
    N, D = x.shape
    RT = -(-N // P)
    NP = RT * P
    LAST = N - (RT - 1) * P
    KC = D // P
    S = w_sel_x.shape[2]
    G = 4
    SUB = D // P
    EC = src_main.shape[1]
    ET = src_tail.shape[0]
    ECP = -(-(EC + 1) // 2) * 2
    NN = NP * NP
    CW = NN // P + 1
    ITERS = 10
    COLS = [(c, min(512, NP - c)) for c in range(0, NP, 512)]
    TB = 250
    SG = S * G
    CHUNKS = (N // TB - 1) * SG
    TG = 25
    NBLK = N // TG
    EPS = 1e-5
    WARM = 5
    A, B = 11, 13
    GATE_SCALE = float(2 ** (A + B + 1))
    WB = 4
    WIT = S * KC * 2 // WB

    adj = [nc.dram_tensor(f"adjacency_{b}", (P * CW,), f32, kind="Internal").ap() for b in range(2)]
    gx_dram = nc.dram_tensor("gate_inputs", (SG, P, N, SUB), f32, kind="Internal").ap()
    lx_dram = nc.dram_tensor("logit_inputs", (NP, S), f32, kind="Internal").ap()
    pick_dram = nc.dram_tensor("guessed_sets", (NP,), i32, kind="Internal").ap()
    x1_dram = nc.dram_tensor("x1_rows", (NP, D), f32, kind="Internal").ap()

    ctx = ExitStack()
    with ctx:
        def sb(name, shape, dt, where=ctx):
            return where.enter_context(nc.sbuf_tensor(name, shape, dt))

        def sem(name):
            return ctx.enter_context(nc.semaphore(name))

        ident = sb("ident", [P, P], f32)
        ones = sb("ones", [P, P], f32)
        xT = sb("xT", [P, KC, NP], f32)
        scal = sb("scal", [1, 3 + S], f32)
        scal_b = sb("scal_b", [P, 3 + S], f32)
        ab = sb("ab", [P, 4], f32)
        stats = sb("stats", [P, RT, 6], f32)
        mv = sb("mv", [P, RT, 2], f32)
        rstd = sb("rstd", [P, RT], f32)
        square = sb("square", [P, RT], f32)
        root = sb("root", [P, RT], f32)
        newton = sb("newton", [P, RT], f32)
        ramp = sb("ramp", [P, S], f32)
        biases = sb("biases", [P, S * G * SUB], f32)
        bias2 = sb("bias2", [P, S * G * SUB], f32)
        gscale = sb("gscale", [P, S * G * SUB], f32)
        wselx = sb("wselx", [P, KC, S], f32)
        wsel = sb("wsel", [P, S, 2 * SUB], f32)
        lx_t = sb("lx_t", [P, RT, S], f32)
        lx_w = sb("lx_w", [P, RT, S], f32)
        lx_m = sb("lx_m", [P, RT], f32)
        pick_t = sb("pick_t", [P, RT], i32)
        with ExitStack() as graph:
            X = sb("X", [P, RT, D], f32, graph)
            O0 = sb("O0", [P, RT, D], f32, graph)
            O1 = sb("O1", [P, RT, D], f32, graph)
            Adj = sb("Adj", [P, RT, NP], f32, graph)
            Adj1 = sb("Adj1", [P, CW], f32, graph)
            sim = sb("sim", [P, 2, NP], f32, graph)
            not_ident = sb("not_ident", [P, P], f32, graph)
            below = sb("below", [P, P], f32, graph)
            src_i = sb("src_i", [P, ECP], i32, graph)
            dst_i = sb("dst_i", [P, ECP], i32, graph)
            src_f = sb("src_f", [P, ECP], f32, graph)
            dst_f = sb("dst_f", [P, ECP], f32, graph)
            ew = sb("ew", [P, ECP], f32, graph)
            key = sb("key", [P, ECP], f32, graph)
            to_dump = sb("to_dump", [P, ECP], f32, graph)
            dump_i = sb("dump_i", [P, 1], i32, graph)
            dump_f = sb("dump_f", [P, 1], f32, graph)
            kdiag = sb("kdiag", [P, 2, P], f32, graph)
            same = sb("same", [P, 2, P], f32, graph)
            junk = sb("junk", [P, 2, P], f32, graph)
            earlier = sb("earlier", [P, 2], f32, graph)
            shift = sb("shift", [P, 2], f32, graph)
            total = sb("total", [P, 2, 1], f32, graph)
            where_ = sb("where_", [P, 2, 1], u32, graph)
            sumsq = sb("sumsq", [P, RT], f32, graph)
            den = sb("den", [P, RT], f32, graph)
            adn = sb("adn", [P, RT], f32, graph)
            bdn = sb("bdn", [P, RT], f32, graph)
        XB = Adj1[:, 0:RT * D].rearrange("p (t d) -> p t d", t=RT)

        WH = sb("WH", [P, S * KC, 2, 4, D], f16)
        with ExitStack() as project:
            wst = sb("wst", [P, WB, 2, D], f32, project)
            wih = sb("wih", [P, G, KC, D], f32, project)
            gstage = sb("gstage", [P, 2, TB, SUB], f32, project)
        gateT = sb("gateT", [P, G * SUB, 33], f32)
        gates = sb("gates", [P, G * SUB], f32)
        acts = sb("acts", [P, G * SUB + SUB], f32)
        cprod = sb("cprod", [P, 2 * SUB], f32)
        osig = sb("osig", [P, SUB], f32)
        tanc = sb("tanc", [P, SUB], f32)
        hfull = sb("hfull", [P, SUB], f32)
        hparts = sb("hparts", [P, SUB, 17], f16)
        lprod = sb("lprod", [P, S, 2 * SUB + 1], f32)
        lpart = sb("lpart", [P, S], f32)
        lmax = sb("lmax", [1, 1], f32)
        lmark = sb("lmark", [1, S], f32)
        pick = sb("pick", [1, 1], i32)
        hist = xT
        gblk = sb("gblk", [P, 2, SG, TG, SUB], f32)
        wih_next = sb("wih_next", [P, SUB, KC, P], f32)
        gx_next = sb("gx_next", [P, 2, TB, SUB], f32)
        lx_row = sb("lx_row", [1, NP, S], f32)
        pick_row = sb("pick_row", [1, NP], i32)
        x1_t = wih_next[:, 0:2, :, :].rearrange("p b k n -> p b (k n)")
        out_t = wih_next[:, 2:4, :, :].rearrange("p b k n -> p b (k n)")

        ps = ctx.enter_context(nc.psum_tensor("ps", [P, 8, 512], f32))
        gate_ps = ps[:, 0, :]
        logit_ps = ps[0:1, 1, 0:S]
        seal_ps = ps[0:1, 2, 0:1]
        unit_ps = ps[:, 3, 0:TB]

        x_in = sem("x_in")
        square_ready = sem("square_ready")
        root_ready = sem("root_ready")
        edges_in = sem("edges_in")
        adj_zeroed = sem("adj_zeroed")
        places_free = [sem(f"places_free{b}") for b in range(2)]
        small_in = sem("small_in")
        zero_set = sem("zero_set")
        consts = sem("consts")
        masks = sem("masks")
        v = sem("v")
        a = sem("a")
        scal_mm = sem("scal_mm")
        ab_ready = sem("ab_ready")
        xn_ready = sem("xn_ready")
        trans_mm = sem("trans_mm")
        trans_out = sem("trans_out")
        edge_ready = sem("edge_ready")
        kd_ready = [sem(f"kd_ready{b}") for b in range(2)]
        kr_ready = [sem(f"kr_ready{b}") for b in range(2)]
        same_ready = [sem(f"same_ready{b}") for b in range(2)]
        earlier_ready = [sem(f"earlier_ready{b}") for b in range(2)]
        shift_ready = [sem(f"shift_ready{b}") for b in range(2)]
        total_mm = [sem(f"total_mm{b}") for b in range(2)]
        edge_out = [sem(f"edge_out{b}") for b in range(2)]
        places_ready = [sem(f"places_ready{b}") for b in range(2)]
        prop_ready = sem("prop_ready")
        scattered = [sem(f"scattered{b}") for b in range(2)]
        adj_in = sem("adj_in")
        adj_sum = sem("adj_sum")
        sim_mm = sem("sim_mm")
        sim_masked = sem("sim_masked")
        sim_exp = sem("sim_exp")
        adj_ready = sem("adj_ready")
        deg_mm = sem("deg_mm")
        prop_mm = sem("prop_mm")
        o_part = sem("o_part")
        o_ready = sem("o_ready")
        x1_ready = sem("x1_ready")
        x1_out = sem("x1_out")
        y_ready = sem("y_ready")
        lx_mm = sem("lx_mm")
        lx_ready = sem("lx_ready")
        lx_out = sem("lx_out")
        graph_free = sem("graph_free")
        wih_in = [sem(f"wih_in{g}") for g in range(G)]
        proj_mm = sem("proj_mm")
        proj_out = sem("proj_out")
        gx_stored = sem("gx_stored")
        whh_in = [sem(f"whh_in{b}") for b in range(WB)]
        whh_scaled = [sem(f"whh_scaled{b}") for b in range(WB)]
        whh_high = [sem(f"whh_high{b}") for b in range(WB)]
        whh_low = [sem(f"whh_low{b}") for b in range(WB)]
        wih_next_in = sem("wih_next_in")
        unit_mm = sem("unit_mm")
        unit_out = sem("unit_out")
        rows_in = sem("rows_in")
        gblk_in = [sem(f"gblk_in{b}") for b in range(2)]
        lx0_set = sem("lx0_set")
        lx_next = sem("lx_next")
        hist_free = sem("hist_free")
        h_ready = sem("h_ready")
        lpart_ready = sem("lpart_ready")
        logits_mm = sem("logits_mm")
        lmax_ready = sem("lmax_ready")
        lmark_ready = sem("lmark_ready")
        pick_ready = sem("pick_ready")
        scatter_seen = sem("scatter_seen")
        stage_seen = sem("stage_seen")
        pick_seen = sem("pick_seen")
        gates_mm = sem("gates_mm")
        turned = sem("turned")
        gx_set = sem("gx_set")
        gates_ready = sem("gates_ready")
        acts_ready = sem("acts_ready")
        cprod_ready = sem("cprod_ready")
        osig_ready = sem("osig_ready")
        c_ready = sem("c_ready")
        tanc_ready = sem("tanc_ready")
        h_full = sem("h_full")
        lprod_c = sem("lprod_c")
        lprod_h = sem("lprod_h")
        x1_back = [sem(f"x1_back{b}") for b in range(2)]
        out_mm = sem("out_mm")
        out_sum = sem("out_sum")
        out_done = [sem(f"out_done{b}") for b in range(2)]

        EIT = ECP // 2
        NCH = len(COLS)
        TQ = [(q, min(4, RT - q)) for q in range(0, RT, 4)]
        NTQ = KC * len(TQ)

        block = ctx.enter_context(nc.Block())

        @block.sync
        def _(sp):
            sp.wait_ge(zero_set, 1)
            sp.dma_start(X[:, 0:RT - 1, :], x[0:(RT - 1) * P, :].rearrange("(t p) d -> p t d", p=P)).then_inc(x_in, 16)
            sp.dma_start(X[0:LAST, RT - 1, :], x[(RT - 1) * P:N, :]).then_inc(x_in, 16)
            sp.wait_ge(zero_set, 2)
            for b in range(2):
                sp.dma_start(adj[b].rearrange("(p n) -> p n", p=P), Adj1[:, :]).then_inc(adj_zeroed, 16)
            for b in range(2):
                sp.wait_ge(scattered[b], 16 * EIT)
            sp.dma_start(Adj[:, :, :], adj[0][0:NN].rearrange("(t p n) -> p t n", p=P, n=NP)).then_inc(adj_in, 16)
            sp.dma_start(Adj1[:, 0:RT * NP].rearrange("p (t n) -> p t n", t=RT),
                         adj[1][0:NN].rearrange("(t p n) -> p t n", p=P, n=NP)).then_inc(adj_in, 16)
            sp.wait_ge(x1_ready, 1)
            sp.dma_start(x1_dram.rearrange("(t p) d -> p t d", p=P), X[:, :, :]).then_inc(x1_out, 16)
            sp.wait_ge(lx_ready, 1)
            sp.dma_start(lx_dram.rearrange("(t p) s -> p t s", p=P), lx_t[:, :, :]).then_inc(lx_out, 16)
            sp.dma_start(pick_dram.rearrange("(t p) -> p t", p=P), pick_t[:, :], allow_slow_non_contiguous=True).then_inc(lx_out, 16)
            sp.wait_ge(x1_out, 16)
            sp.wait_ge(graph_free, 1)
            for g in range(G):
                sp.dma_start(wih[:, g, :, :].rearrange("p k n -> p (k n)"), w_ih[:, 0, g, :]).then_inc(wih_in[g], 16)

            def store(s, g):
                taken = sp.snap(s * (G * SUB) + (g * SUB + SUB + 8))
                landed = sp.snap(s * (16 * G) + (16 * g + 32))
                chunk = sp.snap(s * G + g)
                sp.wait_ge(proj_out, taken)
                sp.sem_inc(stage_seen, 1)
                sp.wait_ge(gx_stored, landed)
                sp.dma_start(gx_dram[bass.ds(chunk, 1), :, 0:TB, :].rearrange("a p t c -> p (a t c)"),
                             gstage[:, g % 2, :, :].rearrange("p t c -> p (t c)")).then_inc(gx_stored, 16)

            with sp.Fori(0, S - 1) as s:
                for g in range(G):
                    sp.wait_ge(proj_mm, sp.snap(s * (G * SUB) + (g + 1) * SUB))
                    sp.dma_start(wih[:, g, :, :].rearrange("p k n -> p (k n)"),
                                 w_ih[:, bass.ds(s + 1, 1), g, :].rearrange("p a n -> p (a n)")).then_inc(wih_in[g], 16)
                    store(s, g)
            for g in range(G):
                store(sp.snap(S - 1), g)
            sp.wait_ge(gx_stored, 16 * (SG + 2))
            sp.wait_ge(lx_out, 32)
            for b in range(WB):
                sp.wait_ge(whh_low[b], WIT + 1)
            sp.dma_start(lx_row[0:1, :, :], lx_dram.rearrange("(a t) s -> a t s", a=1)).then_inc(rows_in, 16)
            sp.dma_start(pick_row[0:1, :], pick_dram.rearrange("(a t) -> a t", a=1)).then_inc(rows_in, 16)
            for b in range(2):
                sp.dma_start(gblk[:, b, :, :, :].rearrange("p s t c -> p s (t c)"),
                             gx_dram[:, :, b * TG:(b + 1) * TG, :].rearrange("s p t c -> p s (t c)")).then_inc(gblk_in[b], 16)
            w_units = w_ih.rearrange("p s g (k u n) -> p (s g) k u n", k=KC, u=SUB)

            def load_unit(c, u):
                sp.dma_start(wih_next[:, bass.ds(u, 1), :, :].rearrange("p a k n -> p (a k) n"),
                             w_units[:, bass.ds(c % SG, 1), :, bass.ds(u, 1), :].rearrange("p a k u n -> p (a k) (u n)")
                             ).then_inc(wih_next_in, 16)

            def store_chunk(c):
                sp.wait_ge(unit_out, sp.snap(c * SUB + (SUB + 1)))
                sp.wait_ge(gx_stored, sp.snap(c * 16 + 16 * (SG + 2)))
                sp.dma_start(gx_dram[bass.ds(c % SG, 1), :, bass.ds((c // SG) * TB + TB, TB), :].rearrange("a p t c -> p (a t c)"),
                             gx_next[:, bass.ds(c % 2, 1), :, :].rearrange("p a t c -> p (a t c)")).then_inc(gx_stored, 16)

            for u in range(SUB):
                load_unit(sp.snap(0), u)
                sp.wait_ge(wih_next_in, 16 * (u + 1))
            with sp.Fori(0, CHUNKS - 1) as c:
                with sp.Fori(0, SUB) as u:
                    t = sp.snap(c * SUB + u)
                    sp.wait_ge(unit_mm, sp.snap(t + 1))
                    sp.wait_ge(wih_next_in, sp.snap(t * 16 + 16 * SUB))
                    load_unit(sp.snap(c + 1), u)
                store_chunk(c)
            store_chunk(sp.snap(CHUNKS - 1))
            sp.wait_ge(unit_mm, CHUNKS * SUB)
            sp.wait_ge(wih_next_in, 16 * CHUNKS * SUB)
            sp.wait_ge(gx_stored, 16 * (SG + 2 + CHUNKS))
            for t in range(RT):
                b = t % 2
                if t >= 2:
                    sp.wait_ge(out_sum, SUB * (t - 1))
                sp.dma_start(x1_t[:, b, :], x1_dram[t * P:(t + 1) * P, :]).then_inc(x1_back[b], 16)
            for b in range(2):
                sp.wait_ge(out_done[b], 16 * (RT // 2))

        @block.gpsimd
        def _(pool):
            pool.wait_ge(consts, 1)
            pool.affine_select(out=below[:, :], in_=ones[:, :], compare_op=ALU.is_gt, fill=0.0, base=0,
                               pattern=[[-1, P]], channel_multiplier=1).then_inc(masks, 1)
            pool.affine_select(out=not_ident[:, :], in_=ones[:, :], compare_op=ALU.not_equal, fill=0.0, base=0,
                               pattern=[[-1, P]], channel_multiplier=1).then_inc(masks, 1)
            pool.wait_ge(consts, 2)
            pool.affine_select(out=ident[:, :], in_=ident[:, :], compare_op=ALU.not_equal, fill=1.0, base=0,
                               pattern=[[-1, P]], channel_multiplier=1).then_inc(masks, 1)
            pool.iota(dump_i[:, :], pattern=[[0, 1]], base=NN, channel_multiplier=1).then_inc(masks, 1)
            last_word = pool.alloc_register("last_word")
            pool.reg_mov(last_word, P * CW - 1)
            pool.wait_ge(adj_zeroed, 32)
            for b in range(2):
                pool.sem_inc(places_free[b], 1)
            with pool.Fori(0, EIT) as i:
                n = pool.snap(i + 1)
                n16 = pool.snap(i * 16 + 16)
                for b in range(2):
                    pool.wait_ge(places_ready[b], n)
                    pool.wait_ge(edge_out[b], n)
                    pool.sem_inc(scatter_seen, 1)
                    pool.indirect_dma_start(
                        out=adj[b].rearrange("(n a) -> n a", a=1),
                        out_offset=bass.IndirectOffsetOnAxis(ap=where_[:, b, :], axis=0),
                        in_=total[:, b, :], in_offset=None, compute_op=ALU.add,
                        bounds_check=last_word, oob_is_err=True).then_inc(scattered[b], 16)
                for b in range(2):
                    pool.wait_ge(scattered[b], n16)
                    pool.sem_inc(places_free[b], 1)
            for b in range(WB):
                pool.sem_inc(whh_low[b], 1)
            with pool.Fori(0, WIT) as i:
                n = pool.snap(i + 1)
                for b in range(WB):
                    j = 2 * (b % 2)
                    chunk = bass.ds(i * (WB // 2) + b // 2, 1)
                    pool.wait_ge(whh_high[b], n)
                    pool.tensor_tensor(WH[:, chunk, 1, j:j + 2, :].rearrange("p a j n -> p (a j n)"),
                                       wst[:, b, :, :].rearrange("p j n -> p (j n)"),
                                       WH[:, chunk, 0, j:j + 2, :].rearrange("p a j n -> p (a j n)"),
                                       ALU.subtract).then_inc(whh_low[b], 1)
            pool.wait_ge(rows_in, 32)
            pool.wait_ge(lx_ready, 2)
            pool.tensor_copy(lprod[0:1, :, 2 * SUB], lx_row[0:1, 0, :]).then_inc(lx0_set, 1)

            def side_steps(t, n, n2):
                pool.wait_ge(lpart_ready, n)
                pool.tensor_copy(lprod[0:1, :, 2 * SUB:2 * SUB + 1].rearrange("a s c -> a (s c)"),
                                 lx_row[0:1, bass.ds(t + 1, 1), :].rearrange("a t s -> a (t s)")).then_inc(lx_next, 1)
                pool.wait_ge(h_full, n2)
                pool.tensor_copy(hist[:, :, bass.ds(t, 1)].rearrange("p s t -> p (s t)"), hfull[:, :]).then_inc(hist_free, 1)

            with pool.Fori(0, N) as t:
                side_steps(t, pool.snap(t + 1), pool.snap(t * 2 + 2))

        @block.scalar
        def _(act):
            chain = [0]

            def link(ins):
                chain[0] += 1
                ins.then_inc(a, 1)
                act.wait_ge(a, chain[0])

            act.dma_start(scal[:, :], scalars).then_inc(small_in, 16)
            act.dma_start(biases[:, :], b_ih).then_inc(small_in, 16)
            act.dma_start(bias2[:, :], b_hh).then_inc(small_in, 16)
            act.dma_start(wselx[:, :, :], w_sel_x).then_inc(small_in, 16)
            act.dma_start(wsel[:, :, :], w_sel_state).then_inc(small_in, 16)
            act.wait_ge(edge_ready, 1)
            for tile, main, tail in ((src_i, src_main, src_tail), (dst_i, dst_main, dst_tail), (ew, ew_main, ew_tail)):
                act.dma_start(tile[:, 0:EC], main).then_inc(edges_in, 16)
                act.dma_start(tile[0:ET, EC:EC + 1], tail).then_inc(edges_in, 16)
            act.wait_ge(scal_mm, 2)
            act.activation(ab[:, 0:2], scal_b[:, 0:2], ACT.Exp).then_inc(ab_ready, 1)
            act.activation(ab[:, 2:3], scal_b[:, 2:3], ACT.Exp, scale=-2.0).then_inc(ab_ready, 1)

            def take_root(n):
                act.wait_ge(square_ready, n)
                act.activation(root[:, :], square[:, :], ACT.Sqrt).then_inc(root_ready, 1)

            take_root(1)
            take_root(2)

            def evacuate_transposes(first):
                for k in range(KC):
                    for q, (r0, m) in enumerate(TQ):
                        i = first + k * len(TQ) + q
                        act.wait_ge(trans_mm, i + 1)
                        act.activation(xT[:, k, r0 * P:(r0 + m) * P], ps[:, i % 8, 0:m * P], ACT.Copy).then_inc(trans_out, 1)

            evacuate_transposes(0)
            act.wait_ge(ab_ready, 3)
            for r in range(RT):
                for c, (c0, m) in enumerate(COLS):
                    act.wait_ge(sim_mm, NCH * r + c + 1)
                    if c0 <= r * P < c0 + m:
                        act.wait_ge(sim_masked, r + 1)
                    if r >= 2:
                        act.wait_ge(adj_ready, r - 1)
                    act.activation(sim[:, r % 2, c0:c0 + m], ps[:, 2 + 3 * (r % 2) + c, 0:m], ACT.Exp,
                                   scale=ab[:, 3:4]).then_inc(sim_exp, 1)
            take_root(3)
            evacuate_transposes(NTQ)
            act.wait_ge(x1_out, 16)
            act.wait_ge(graph_free, 1)
            w_v = w_hh.rearrange("p (c b n) -> p c b n", c=S * KC, b=2)

            def load_half(i, b):
                act.wait_ge(whh_low[b], act.snap(i + 1))
                act.dma_start(wst[:, b, :, :].rearrange("p j n -> p (j n)"),
                              w_v[:, bass.ds(i * (WB // 2) + b // 2, 1), b % 2, :].rearrange("p a n -> p (a n)")).then_inc(whh_in[b], 16)

            def split_halves(i, more):
                for b in range(WB):
                    j = 2 * (b % 2)
                    if b + 2 < WB:
                        load_half(i, b + 2)
                    elif more:
                        load_half(act.snap(i + 1), b + 2 - WB)
                    act.wait_ge(whh_in[b], act.snap(i * 16 + 16))
                    act.activation(wst[:, b, :, 0:3 * P], wst[:, b, :, 0:3 * P], ACT.Copy, scale=float(2 ** (A - 1))).then_inc(whh_scaled[b], 1)
                    act.activation(wst[:, b, :, 3 * P:D], wst[:, b, :, 3 * P:D], ACT.Copy, scale=float(2 ** A)).then_inc(whh_scaled[b], 1)
                    act.wait_ge(whh_scaled[b], act.snap(i * 2 + 2))
                    act.activation(WH[:, bass.ds(i * (WB // 2) + b // 2, 1), 0, j:j + 2, :].rearrange("p a j n -> p (a j n)"),
                                   wst[:, b, :, :].rearrange("p j n -> p (j n)"), ACT.Copy).then_inc(whh_high[b], 1)

            for b in range(2):
                load_half(act.snap(0), b)
            with act.Fori(0, WIT - 1) as i:
                split_halves(i, True)
            split_halves(act.snap(WIT - 1), False)
            act.activation(root[:, :], square[:, :], ACT.Tanh)
            def act_block(i, b, stored):
                act.wait_ge(gblk_in[b], act.snap(i * 16 + 16))
                with act.Fori(0, TG) as tl:
                    n = act.snap(i * (2 * TG) + tl + (b * TG + 1))
                    act.wait_ge(pick_ready, n)
                    act.sem_inc(pick_seen, 1)
                    r = act.value_load(pick[0:1, 0:1], min_val=1, max_val=S)
                    act.activation(gateT[:, :, 32:33].rearrange("p (g c) a -> p g (c a)", g=G),
                                   gblk[:, b, bass.ds(r * G - G, G), bass.ds(tl, 1), :].rearrange("p s t c -> p s (t c)"),
                                   ACT.Copy).then_inc(gx_set, 1)
                    act.wait_ge(gates_ready, n)
                    act.activation(acts[:, 0:G * SUB], gates[:, :], ACT.Tanh, scale=1.0 / GATE_SCALE).then_inc(acts_ready, 1)
                    act.wait_ge(c_ready, n)
                    act.activation(tanc[:, :], acts[:, G * SUB:G * SUB + SUB], ACT.Tanh, scale=0.5).then_inc(tanc_ready, 1)
                if stored is not None:
                    act.wait_ge(gx_set, act.snap(i * (2 * TG) + (b + 1) * TG))
                    act.wait_ge(gx_stored, stored)
                    act.dma_start(gblk[:, b, :, :, :].rearrange("p s t c -> p s (t c)"),
                                  gx_dram[:, :, bass.ds(i * (2 * TG) + (b + 2) * TG, TG), :].rearrange("s p t c -> p s (t c)")
                                  ).then_inc(gblk_in[b], 16)

            ahead = -(-CHUNKS * SUB // (2 * TG)) - 1
            with act.Fori(0, ahead) as i:
                stored = act.snap(i * (16 * SG // (TB // (2 * TG) - 1)) + 16 * (SG + 2))
                for b in range(2):
                    act_block(i, b, stored)
            with act.Fori(ahead, NBLK // 2 - 1) as i:
                for b in range(2):
                    act_block(i, b, 16 * (SG + 2 + CHUNKS))
            for b in range(2):
                act_block(act.snap(NBLK // 2 - 1), b, None)
            for t in range(RT):
                b = t % 2
                rows = P if t < RT - 1 else LAST
                act.wait_ge(out_sum, SUB * (t + 1))
                act.dma_start(out[t * P:t * P + rows, :], out_t[0:rows, b, :]).then_inc(out_done[b], 16)

        @block.vector
        def _(dve):
            chain = [0]

            def link(ins):
                chain[0] += 1
                ins.then_inc(v, 1)
                dve.wait_ge(v, chain[0])

            dve.memset(X[:, RT - 1, :], 0.0).then_inc(zero_set, 1)
            dve.memset(Adj1[:, :], 0.0).then_inc(zero_set, 1)
            dve.memset(ones[:, :], 1.0).then_inc(consts, 1)
            dve.memset(ident[:, :], 0.0).then_inc(consts, 1)
            dve.memset(src_i[:, :], 0)
            dve.memset(dst_i[:, :], 0)
            dve.memset(ew[:, :], 0.0).then_inc(edge_ready, 1)
            for s in range(S):
                link(dve.memset(ramp[:, s:s + 1], float(S - s)))

            dve.wait_ge(scal_mm, 1)
            dve.tensor_copy(scal_b[:, :], ps[:, 7, 0:3 + S]).then_inc(scal_mm, 1)
            dve.wait_ge(ab_ready, 2)
            dve.tensor_scalar(ab[:, 3:4], ab[:, 2:3], 0.25, None, ALU.mult).then_inc(ab_ready, 1)

            roots = [0]

            def inverse_root(to):
                roots[0] += 1
                dve.sem_inc(square_ready, 1)
                dve.wait_ge(root_ready, roots[0])
                link(dve.reciprocal(to[:, :], root[:, :]))
                link(dve.tensor_tensor(newton[:, :], to[:, :], to[:, :], ALU.mult))
                link(dve.tensor_tensor(newton[:, :], newton[:, :], square[:, :], ALU.mult))
                link(dve.tensor_scalar(newton[:, :], newton[:, :], -0.5, 1.5, ALU.mult, ALU.add))
                link(dve.tensor_tensor(to[:, :], to[:, :], newton[:, :], ALU.mult))

            def layernorm_stats():
                for r in range(RT):
                    dve.bn_stats(stats[:, r, :], X[:, r, :]).then_inc(v, 1)
                    chain[0] += 1
                dve.wait_ge(v, chain[0])
                for r in range(RT):
                    dve.bn_aggr(mv[:, r, :], stats[:, r, :]).then_inc(v, 1)
                    chain[0] += 1
                dve.wait_ge(v, chain[0])
                link(dve.tensor_scalar(square[:, :], mv[:, :, 1], EPS, None, ALU.add))
                inverse_root(rstd)

            dve.wait_ge(x_in, 32)
            layernorm_stats()
            for r in range(RT):
                link(dve.tensor_scalar(O0[:, r, :], X[:, r, :], mv[:, r, 0:1], rstd[:, r:r + 1], ALU.subtract, ALU.mult))
                link(dve.scalar_tensor_tensor(out=O1[:, r, :], in0=O0[:, r, :], scalar=1.0, in1=O0[:, r, :],
                                              op0=ALU.mult, op1=ALU.mult, accum_out=sumsq[:, r:r + 1]))
            link(dve.tensor_scalar(square[:, :], sumsq[:, :], 1e-12, None, ALU.max))
            inverse_root(sumsq)
            for r in range(RT):
                dve.tensor_scalar(O1[:, r, :], O0[:, r, :], sumsq[:, r:r + 1], None, ALU.mult).then_inc(xn_ready, 1)

            dve.wait_ge(masks, 4)
            link(dve.tensor_copy(dump_f[:, :], dump_i[:, :]))
            dve.wait_ge(edges_in, 16 * 6)
            link(dve.tensor_copy(src_f[:, :], src_i[:, :]))
            link(dve.tensor_copy(dst_f[:, :], dst_i[:, :]))
            for c in range(EC, ECP):
                link(dve.tensor_copy(key[:, c:c + 1], dump_f[:, :]))
            link(dve.scalar_tensor_tensor(out=key[:, 0:EC], in0=dst_f[:, 0:EC], scalar=float(NP), in1=src_f[:, 0:EC],
                                          op0=ALU.mult, op1=ALU.add))
            link(dve.scalar_tensor_tensor(out=key[0:ET, EC:EC + 1], in0=dst_f[0:ET, EC:EC + 1], scalar=float(NP),
                                          in1=src_f[0:ET, EC:EC + 1], op0=ALU.mult, op1=ALU.add))
            link(dve.tensor_scalar(to_dump[:, :], key[:, :], dump_f[:, 0:1], -1.0, ALU.subtract, ALU.mult))
            with dve.Fori(0, EIT) as i:
                n = dve.snap(i + 1)
                kcol = [key[:, bass.ds(i * 2 + b, 1)] for b in range(2)]
                dcol = [to_dump[:, bass.ds(i * 2 + b, 1)] for b in range(2)]
                for b in range(2):
                    dve.tensor_scalar(kdiag[:, b, :], ident[:, :], kcol[b], None, ALU.mult).then_inc(kd_ready[b], 1)
                for b in range(2):
                    dve.wait_ge(kr_ready[b], n)
                    dve.tensor_scalar(same[:, b, :], ps[:, 2 * b, 0:P], kcol[b], None, ALU.is_equal).then_inc(same_ready[b], 1)
                    dve.scalar_tensor_tensor(out=junk[:, b, :], in0=ps[:, 2 * b, 0:P], scalar=kcol[b], in1=below[:, :],
                                             op0=ALU.is_equal, op1=ALU.mult, accum_out=earlier[:, b:b + 1]).then_inc(earlier_ready[b], 1)
                for b in range(2):
                    dve.wait_ge(earlier_ready[b], n)
                    dve.scalar_tensor_tensor(out=shift[:, b:b + 1], in0=earlier[:, b:b + 1], scalar=1.0, in1=dcol[b],
                                             op0=ALU.min, op1=ALU.mult).then_inc(shift_ready[b], 1)
                for b in range(2):
                    dve.wait_ge(shift_ready[b], n)
                    dve.wait_ge(places_free[b], n)
                    dve.tensor_tensor(where_[:, b, :], shift[:, b:b + 1], kcol[b], ALU.add).then_inc(places_ready[b], 1)
                    dve.wait_ge(total_mm[b], n)
                    dve.tensor_copy(total[:, b, :], ps[:, 2 * b + 1, 0:1]).then_inc(edge_out[b], 1)
            dve.wait_ge(adj_in, 32)
            for r in range(RT):
                dve.tensor_tensor(Adj[:, r, :], Adj[:, r, :], Adj1[:, r * NP:(r + 1) * NP], ALU.add).then_inc(adj_sum, 1)
            for r in range(RT):
                c = r // 4
                q = r * P - COLS[c][0]
                dve.wait_ge(sim_mm, NCH * r + c + 1)
                blk = ps[:, 2 + 3 * (r % 2) + c, q:q + P]
                dve.tensor_tensor(blk, blk, not_ident[:, :], ALU.mult).then_inc(sim_masked, 1)
                dve.wait_ge(adj_sum, r + 1)
                dve.wait_ge(sim_exp, NCH * (r + 1))
                dve.tensor_tensor(Adj[:, r, :], Adj[:, r, :], sim[:, r % 2, :], ALU.mult).then_inc(adj_ready, 1)
            dve.wait_ge(deg_mm, 1)
            link(dve.tensor_scalar(den[:, :], ps[:, 0, 0:RT], ab[:, 0:1], ab[:, 1:2], ALU.mult, ALU.add))
            link(dve.tensor_scalar(den[:, :], den[:, :], ab[:, 0:1], None, ALU.add))
            link(dve.reciprocal(den[:, :], den[:, :]))
            link(dve.tensor_scalar(adn[:, :], den[:, :], ab[:, 0:1], None, ALU.mult))
            link(dve.tensor_scalar(bdn[:, :], den[:, :], ab[:, 1:2], None, ALU.mult))
            for r in range(RT):
                link(dve.tensor_scalar(XB[:, r, :], O0[:, r, :], bdn[:, r:r + 1], None, ALU.mult))
            dve.sem_inc(prop_ready, 1)
            with dve.Fori(0, ITERS // 2) as i:
                for half, (old, new) in enumerate(((O0, O1), (O1, O0))):
                    for r in range(RT):
                        dve.scalar_tensor_tensor(out=new[:, r, :], in0=old[:, r, :], scalar=adn[:, r:r + 1], in1=XB[:, r, :],
                                                 op0=ALU.mult, op1=ALU.add).then_inc(o_part, 1)
                    for r in range(RT):
                        n = dve.snap(i * (2 * RT) + (half * RT + r + 1))
                        dve.wait_ge(o_part, n)
                        dve.wait_ge(prop_mm, n)
                        dve.scalar_tensor_tensor(out=new[:, r, :], in0=ps[:, r % 8, :], scalar=adn[:, r:r + 1], in1=new[:, r, :],
                                                 op0=ALU.mult, op1=ALU.add).then_inc(o_ready, 1)
                    dve.wait_ge(o_ready, n)
            dve.wait_ge(o_ready, ITERS * RT)
            for r in range(RT):
                link(dve.tensor_tensor(X[:, r, :], X[:, r, :], O0[:, r, :], ALU.add))
            dve.sem_inc(x1_ready, 1)
            layernorm_stats()
            for r in range(RT):
                dve.tensor_scalar(O1[:, r, :], X[:, r, :], mv[:, r, 0:1], rstd[:, r:r + 1], ALU.subtract, ALU.mult).then_inc(y_ready, 1)
            dve.wait_ge(small_in, 16 * 5)
            dve.wait_ge(lx_mm, 1)
            bsel = scal_b[:, 3:3 + S].rearrange("p (a s) -> p a s", a=1).broadcast_to([P, RT, S])
            link(dve.tensor_tensor(lx_t[:, :, :], ps[:, 0, 0:RT * S].rearrange("p (t s) -> p t s", s=S), bsel, ALU.add))
            link(dve.memset(lx_t[0:1, 0, :], 0.0))
            link(dve.memset(lx_t[0:1, 0, 0:1], 1.0))
            link(dve.tensor_reduce(lx_m[:, :], lx_t[:, :, :], AX.X, ALU.max))
            link(dve.tensor_tensor(lx_w[:, :, :], lx_t[:, :, :], lx_m[:, :].rearrange("p (t a) -> p t a", a=1).broadcast_to([P, RT, S]), ALU.is_ge))
            link(dve.tensor_tensor(lx_w[:, :, :], lx_w[:, :, :], ramp[:, :].rearrange("p (a s) -> p a s", a=1).broadcast_to([P, RT, S]), ALU.mult))
            dve.tensor_reduce(pick_t[:, :], lx_w[:, :, :], AX.X, ALU.max).then_inc(lx_ready, 1)
            link(dve.tensor_tensor(biases[:, :], biases[:, :], bias2[:, :], ALU.add))
            bv = biases[:, :].rearrange("p (s g c) -> p s g c", s=S, g=G)
            link(dve.tensor_scalar(bv[:, :, 0:3, :], bv[:, :, 0:3, :], GATE_SCALE / 2, None, ALU.mult))
            link(dve.tensor_scalar(bv[:, :, 3:4, :], bv[:, :, 3:4, :], GATE_SCALE, None, ALU.mult))
            link(dve.tensor_scalar(wsel[:, :, 0:SUB], wsel[:, :, 0:SUB], 0.5, None, ALU.mult))
            link(dve.tensor_scalar(wsel[:, :, SUB:2 * SUB], wsel[:, :, SUB:2 * SUB], float(2.0 ** -(B + 1)), None, ALU.mult))
            gv = gscale[:, :].rearrange("p (s g c) -> p s g c", s=S, g=G)
            link(dve.memset(gv[:, :, 0:3, :], GATE_SCALE / 2))
            link(dve.memset(gv[:, :, 3:4, :], GATE_SCALE))
            dve.wait_ge(graph_free, 1)
            dve.wait_ge(x1_out, 16)
            dve.sem_inc(proj_out, 8)
            dve.sem_inc(gx_stored, 32)
            with dve.Fori(0, S) as s:
                for c in range(G * SUB):
                    if c % SUB == 0:
                        dve.wait_ge(gx_stored, dve.snap(s * (16 * G) + 16 * (c // SUB + 1)))
                    dve.wait_ge(proj_mm, dve.snap(s * (G * SUB) + (c + 1)))
                    dve.tensor_scalar(gstage[:, c // SUB % 2, :, c % SUB], ps[:, c % 8, 0:TB], GATE_SCALE if c // SUB == 3 else GATE_SCALE / 2,
                                      biases[:, bass.ds(s * (G * SUB) + c, 1)], ALU.mult, ALU.add).then_inc(proj_out, 1)
            for b in range(WB):
                dve.wait_ge(whh_low[b], WIT + 1)
            dve.wait_ge(gx_stored, 16 * (SG + 2))
            dve.wait_ge(proj_mm, S * G * SUB)
            dve.wait_ge(proj_out, S * G * SUB + 8)
            link(dve.memset(gateT[:, :, :], 0.0))
            link(dve.memset(gate_ps, 0.0))
            link(dve.memset(acts[:, G * SUB:G * SUB + SUB], 0.0))
            link(dve.memset(lprod[:, :, :], 0.0))
            dve.sem_inc(lx_ready, 1)
            dve.memset(hparts[:, :, :], 0.0).then_inc(h_ready, 1)
            dve.sem_inc(hist_free, 1)
            dve.wait_ge(lx0_set, 1)
            dve.tensor_reduce(lpart[:, :], lprod[:, :, :], AX.X, ALU.add).then_inc(lpart_ready, 1)

            def choose(n):
                dve.wait_ge(logits_mm, n)
                dve.tensor_reduce(lmax[:, :], logit_ps, AX.X, ALU.max).then_inc(lmax_ready, 1)
                dve.wait_ge(lmax_ready, n)
                dve.scalar_tensor_tensor(out=lmark[:, :], in0=logit_ps, scalar=lmax[:, 0:1], in1=ramp[0:1, :],
                                         op0=ALU.is_ge, op1=ALU.mult).then_inc(lmark_ready, 1)
                dve.wait_ge(lmark_ready, n)
                dve.tensor_reduce(pick[:, :], lmark[:, :], AX.X, ALU.max).then_inc(pick_ready, 1)

            def cell(n, n2):
                dve.wait_ge(gates_mm, n)
                dve.transpose(gateT[:, :, 0:32], gate_ps.rearrange("p (c q) -> p c q", q=32)).then_inc(turned, 1)
                dve.wait_ge(turned, n)
                dve.wait_ge(gx_set, n)
                dve.tensor_reduce(gates[:, :], gateT[:, :, 0:33:16], AX.X, ALU.add).then_inc(gates_ready, 1)
                dve.wait_ge(acts_ready, n)
                dve.scalar_tensor_tensor(out=cprod[:, :], in0=acts[:, 0:2 * SUB], scalar=1.0, in1=acts[:, 3 * SUB:5 * SUB],
                                         op0=ALU.add, op1=ALU.mult).then_inc(cprod_ready, 1)
                dve.tensor_scalar(osig[:, :], acts[:, 2 * SUB:3 * SUB], 1.0, float(2 ** B), ALU.add, ALU.mult).then_inc(osig_ready, 1)
                dve.wait_ge(cprod_ready, n)
                dve.scalar_tensor_tensor(out=acts[:, 4 * SUB:5 * SUB], in0=cprod[:, SUB:2 * SUB], scalar=0.5, in1=cprod[:, 0:SUB],
                                         op0=ALU.mult, op1=ALU.add).then_inc(c_ready, 1)
                dve.wait_ge(osig_ready, n)
                dve.wait_ge(lx_next, n)
                dve.wait_ge(hist_free, n)
                dve.wait_ge(c_ready, n)
                dve.tensor_tensor(lprod[:, :, 0:SUB], acts[:, 4 * SUB:5 * SUB].rearrange("p (a c) -> p a c", a=1).broadcast_to([P, S, SUB]),
                                  wsel[:, :, 0:SUB], ALU.mult).then_inc(lprod_c, 1)
                dve.wait_ge(tanc_ready, n)
                dve.tensor_tensor(hfull[:, :], osig[:, :], tanc[:, :], ALU.mult).then_inc(h_full, 1)
                dve.tensor_tensor(hparts[:, :, 0], osig[:, :], tanc[:, :], ALU.mult).then_inc(h_full, 1)
                dve.wait_ge(h_full, n2)
                dve.tensor_tensor(hparts[:, :, 16], hfull[:, :], hparts[:, :, 0], ALU.subtract).then_inc(h_ready, 1)

            def logit_parts(n):
                dve.wait_ge(lprod_c, n)
                dve.tensor_tensor(lprod[:, :, SUB:2 * SUB], hfull[:, :].rearrange("p (a c) -> p a c", a=1).broadcast_to([P, S, SUB]),
                                  wsel[:, :, SUB:2 * SUB], ALU.mult).then_inc(lprod_h, 1)
                dve.wait_ge(lprod_h, n)
                dve.tensor_reduce(lpart[:, :], lprod[:, :, :], AX.X, ALU.add).then_inc(lpart_ready, 1)

            choose(1)
            dve.sem_inc(unit_out, 1)

            def step(t):
                n = dve.snap(t + 1)
                cell(n, dve.snap(t * 2 + 2))
                logit_parts(n)
                choose(dve.snap(t + 2))
                return n

            with dve.Fori(0, CHUNKS) as c:
                with dve.Fori(0, SUB) as u:
                    n = step(dve.snap(c * SUB + u))
                    column = dve.snap((c % SG) * SUB + u)
                    dve.wait_ge(gx_stored, dve.snap(c * 16 + 16 * (SG + 1)))
                    dve.wait_ge(unit_mm, n)
                    dve.tensor_scalar(gx_next[:, bass.ds(c % 2, 1), :, bass.ds(u, 1)].rearrange("p a t c -> p (a t c)"), unit_ps,
                                      gscale[:, bass.ds(column, 1)], biases[:, bass.ds(column, 1)],
                                      ALU.mult, ALU.add).then_inc(unit_out, 1)
            with dve.Fori(CHUNKS * SUB, N - 1) as t:
                step(t)
            cell(N, 2 * N)
            for t in range(RT):
                b = t % 2
                rows = P if t < RT - 1 else LAST
                if t >= 2:
                    dve.wait_ge(out_done[b], 16 * (t // 2))
                dve.wait_ge(x1_back[b], 16 * (t // 2 + 1))
                dve.wait_ge(out_mm, t + 1)
                x1_v = x1_t[0:rows, b, :].rearrange("p (j s q) -> p s j q", j=4, s=SUB)
                out_v = out_t[0:rows, b, :].rearrange("p (j s q) -> p s j q", j=4, s=SUB)
                for s in range(SUB):
                    dve.scalar_tensor_tensor(out=out_v[:, s, :, :],
                                             in0=ps[0:rows, 2 + b, s * P:(s + 1) * P].rearrange("p (j q) -> p j q", j=4),
                                             scalar=float(2.0 ** -(B + 1)), in1=x1_v[:, s, :, :],
                                             op0=ALU.mult, op1=ALU.add).then_inc(out_sum, 1)

        @block.tensor
        def _(pe):
            pe.wait_ge(consts, 1)
            pe.wait_ge(small_in, 16 * 5)
            nc.tensor.matmul(ps[:, 7, 0:3 + S], ones[0:1, :], scal[0:1, :], start=True, stop=True).then_inc(scal_mm, 1)
            pe.wait_ge(masks, 4)
            pe.wait_ge(scal_mm, 2)

            def transposes(src, first, ready, want):
                for k in range(KC):
                    for q, (r0, m) in enumerate(TQ):
                        i = first + k * len(TQ) + q
                        if i >= 8:
                            pe.wait_ge(trans_out, i - 7)
                        for r in range(r0, r0 + m):
                            if k == 0:
                                pe.wait_ge(ready, r + 1)
                            last = nc.tensor.transpose(ps[:, i % 8, (r - r0) * P:(r - r0 + 1) * P],
                                                       src[:, r, k * P:(k + 1) * P], ident[:, :])
                        last.then_inc(trans_mm, 1)

            transposes(O1, 0, xn_ready, 0)
            pe.wait_ge(trans_out, NTQ)
            with pe.Fori(0, EIT) as i:
                n = pe.snap(i + 1)
                for b in range(2):
                    pe.wait_ge(kd_ready[b], n)
                    nc.tensor.matmul(ps[:, 2 * b, 0:P], ones[:, :], kdiag[:, b, :], start=True, stop=True).then_inc(kr_ready[b], 1)
                for b in range(2):
                    pe.wait_ge(same_ready[b], n)
                    nc.tensor.matmul(ps[:, 2 * b + 1, 0:1], same[:, b, :], ew[:, bass.ds(i * 2 + b, 1)],
                                     start=True, stop=True).then_inc(total_mm[b], 1)
            pe.wait_ge(edge_out[0], EIT)
            pe.wait_ge(edge_out[1], EIT)
            for r in range(RT):
                for c, (c0, m) in enumerate(COLS):
                    if r >= 2:
                        pe.wait_ge(sim_exp, NCH * (r - 2) + c + 1)
                    for k in range(KC):
                        last = nc.tensor.matmul(ps[:, 2 + 3 * (r % 2) + c, 0:m], xT[:, k, r * P:(r + 1) * P],
                                                xT[:, k, c0:c0 + m], start=(k == 0), stop=(k == KC - 1))
                    last.then_inc(sim_mm, 1)
            pe.wait_ge(adj_ready, RT)
            for r in range(RT):
                for c in range(RT):
                    last = nc.tensor.matmul(ps[:, 0, r:r + 1], Adj[:, c, r * P:(r + 1) * P], ones[:, 0:1],
                                            start=(c == 0), stop=(c == RT - 1))
            last.then_inc(deg_mm, 1)
            pe.wait_ge(prop_ready, 1)
            with pe.Fori(0, ITERS // 2) as i:
                for half, old in enumerate((O0, O1)):
                    if half == 1:
                        pe.wait_ge(o_ready, pe.snap(i * (2 * RT) + RT))
                    for r in range(RT):
                        if r >= 8:
                            pe.wait_ge(o_ready, pe.snap(i * (2 * RT) + (half * RT + r - 7)))
                        for c in range(RT):
                            last = nc.tensor.matmul(ps[:, r % 8, :], Adj[:, c, r * P:(r + 1) * P], old[:, c, :],
                                                    start=(c == 0), stop=(c == RT - 1))
                        last.then_inc(prop_mm, 1)
                pe.wait_ge(o_ready, pe.snap(i * (2 * RT) + 2 * RT))
            transposes(O1, NTQ, y_ready, 0)
            pe.wait_ge(trans_out, 2 * NTQ)
            pe.sem_inc(graph_free, 1)
            for t in range(RT):
                for k in range(KC):
                    last = nc.tensor.matmul(ps[:, 0, t * S:(t + 1) * S], xT[:, k, t * P:(t + 1) * P], wselx[:, k, :],
                                            start=(k == 0), stop=(k == KC - 1))
            last.then_inc(lx_mm, 1)
            pe.wait_ge(lx_ready, 1)
            with pe.Fori(0, S) as s:
                n16 = pe.snap(s * 16 + 16)
                for g in range(G):
                    pe.wait_ge(wih_in[g], n16)
                    for u in range(SUB):
                        c = g * SUB + u
                        pe.wait_ge(proj_out, pe.snap(s * (G * SUB) + (c + 1)))
                        for k in range(KC):
                            last = nc.tensor.matmul(ps[:, c % 8, 0:TB], wih[:, g, k, u * P:(u + 1) * P],
                                                    xT[:, k, 0:TB], start=(k == 0), stop=(k == KC - 1))
                        last.then_inc(proj_mm, 1)
            for b in range(WB):
                pe.wait_ge(whh_low[b], WIT + 1)

            def products(s, n, first):
                if first:
                    pe.wait_ge(h_ready, n)
                for k in range(KC):
                    for part in range(2):
                        if first and k == 1 and part == 0:
                            pe.wait_ge(lpart_ready, n)
                            nc.tensor.matmul(logit_ps, ones[:, 0:1], lpart[:, :], start=True, stop=True).then_inc(logits_mm, 1)
                        for j in range(4):
                            nc.tensor.matmul(gate_ps[32 * j:32 * j + 17, :], hparts[:, k, :], WH[:, s * KC + k, part, j, :],
                                             start=(k == 0 and part == 0), stop=(k == KC - 1 and part == 1),
                                             tile_position=(0, 32 * j))

            def products_of(chosen, n, first):
                with pe.If_lt(chosen, 3):
                    with pe.If_lt(chosen, 2):
                        products(3, n, first)
                    with pe.Else():
                        products(2, n, first)
                with pe.Else():
                    with pe.If_lt(chosen, 4):
                        products(1, n, first)
                    with pe.Else():
                        products(0, n, first)

            guess = pe.alloc_register("guess")
            chosen = pe.alloc_register("chosen")
            column = pe.alloc_register("column")
            pe.wait_ge(rows_in, 32)
            pe.sem_inc(pick_seen, 1)

            def step(t, n):
                pe.reg_load(guess, pick_row[0:1, bass.ds(t, 1)])
                products_of(guess, n, True)
                pe.wait_ge(pick_ready, n)
                pe.sem_inc(pick_seen, 1)
                pe.reg_load(chosen, pick[0:1, 0:1])
                with pe.If_ne(chosen, guess):
                    products_of(chosen, n, False)
                nc.tensor.matmul(seal_ps, hparts[:, 0, 0:1], hparts[:, 0, 0:1], start=True, stop=True).then_inc(gates_mm, 1)

            def unit(c, u, n, w_in):
                pe.wait_ge(wih_next_in, w_in)
                pe.wait_ge(unit_out, n)
                for k in range(KC):
                    last = nc.tensor.matmul(unit_ps, wih_next[:, u, k, :], xT[:, k, bass.ds((c // SG) * TB + TB, TB)],
                                            start=(k == 0), stop=(k == KC - 1))
                last.then_inc(unit_mm, 1)

            with pe.Fori(0, CHUNKS) as c:
                with pe.Fori(0, SUB) as u:
                    t = pe.snap(c * SUB + u)
                    n = pe.snap(t + 1)
                    step(t, n)
                    w_in = pe.snap(t * 16 + 16)
                    pe.reg_mov(column, u)
                    with pe.If_lt(column, 2):
                        with pe.If_lt(column, 1):
                            unit(c, 0, n, w_in)
                        with pe.Else():
                            unit(c, 1, n, w_in)
                    with pe.Else():
                        with pe.If_lt(column, 3):
                            unit(c, 2, n, w_in)
                        with pe.Else():
                            unit(c, 3, n, w_in)
            with pe.Fori(CHUNKS * SUB, N) as t:
                step(t, pe.snap(t + 1))
                for _ in range(WARM):
                    nc.tensor.matmul(ps[:, 2, :], WH[:, 0, 0, 0, 0:P], WH[:, 0, 0, 0, :], start=True, stop=True)
            pe.wait_ge(hist_free, N + 1)
            for t in range(RT):
                rows = P if t < RT - 1 else LAST
                if t >= 2:
                    pe.wait_ge(out_sum, SUB * (t - 1))
                for s in range(SUB):
                    last = nc.tensor.transpose(ps[0:rows, 2 + t % 2, s * P:(s + 1) * P], hist[:, s, t * P:t * P + rows], ident[:, :])
                last.then_inc(out_mm, 1)


def kernel(**inputs):
    import numpy as np
    import concourse.bacc as bacc
    from concourse import mybir as mb
    from concourse.bass_utils import run_bass_kernel_spmd

    get = {k: np.asarray(val) for k, val in inputs.items()}
    P, D, S = 128, get["x"].shape[1], get["L0_ffn_W_ih"].shape[0]
    edges = get["src"].shape[0]
    main = edges // P * P
    order = [0, 1, 3, 2]

    def cut(a):
        return a[:main].reshape(P, main // P), a[main:].reshape(edges - main, 1)

    def by_unit(a):
        a = a.reshape(S, 4, 4, 4, 32)[::-1, order]
        return a.transpose(2, 4, 0, 1, 3).reshape(P, S * 16)

    whh = get["L0_ffn_W_hh"].reshape(S, 4, 4, P, 4, 4, 32)[:, order]
    whh = whh.transpose(4, 6, 0, 5, 2, 1, 3).reshape(P, S * 4 * 4 * D)
    wih = get["L0_ffn_W_ih"].reshape(S, 4, 4, 4, 32, 4, P)[::-1, order]
    wih = wih.transpose(6, 0, 1, 5, 3, 2, 4).reshape(P, S, 4, 4 * D)
    wsel = get["L0_ffn_W_sel"]
    wsel_h = wsel[:, 0:D].reshape(S, 4, 4, 32).transpose(1, 3, 0, 2).reshape(P, S, 4)
    wsel_c = wsel[:, D:2 * D].reshape(S, 4, 4, 32).transpose(1, 3, 0, 2).reshape(P, S, 4)
    src_main, src_tail = cut(get["src"])
    dst_main, dst_tail = cut(get["dst"])
    ew_main, ew_tail = cut(get["edge_weight"])
    arrays = {
        "x": get["x"],
        "src_main": src_main, "src_tail": src_tail,
        "dst_main": dst_main, "dst_tail": dst_tail,
        "ew_main": ew_main, "ew_tail": ew_tail,
        "scalars": np.concatenate([get["L0_gnn_alpha"], get["L0_gnn_beta"], get["L0_gnn_sigma"], get["L0_ffn_b_sel"]]).reshape(1, 3 + S),
        "w_ih": wih, "w_hh": whh,
        "b_ih": by_unit(get["L0_ffn_b_ih"]), "b_hh": by_unit(get["L0_ffn_b_hh"]),
        "w_sel_state": np.concatenate([wsel_c, wsel_h], axis=2),
        "w_sel_x": wsel[:, 2 * D:3 * D].reshape(S, 4, P).transpose(2, 1, 0),
    }
    nc = bacc.Bacc("TRN2", target_bir_lowering=False, num_devices=1)
    given, args = {}, []
    for name, a in arrays.items():
        a = np.ascontiguousarray(a)
        given[f"in_{name}"] = a
        args.append(nc.dram_tensor(f"in_{name}", a.shape, mb.dt.from_np(a.dtype), kind="ExternalInput").ap())
    out = nc.dram_tensor("out_rows", get["x"].shape, mb.dt.from_np(get["x"].dtype), kind="ExternalOutput").ap()
    gnn_then_selected_lstm(nc, *args, out)
    r = run_bass_kernel_spmd(nc, [given], core_ids=[0])
    return r.results[0]["out_rows"]
```

```python
import concourse.bass as bass
from concourse import mybir
from contextlib import ExitStack


def gnn_then_selected_lstm(
    nc: bass.Bass,
    x: bass.AP,
    src_main: bass.AP,
    src_tail: bass.AP,
    dst_main: bass.AP,
    dst_tail: bass.AP,
    ew_main: bass.AP,
    ew_tail: bass.AP,
    scalars: bass.AP,
    w_ih: bass.AP,
    w_hh: bass.AP,
    b_ih: bass.AP,
    b_hh: bass.AP,
    w_sel_state: bass.AP,
    w_sel_x: bass.AP,
    out: bass.AP,
):
    f32, f16, i32, u32 = mybir.dt.float32, mybir.dt.float16, mybir.dt.int32, mybir.dt.uint32
    ALU, ACT, AX = mybir.AluOpType, mybir.ActivationFunctionType, mybir.AxisListType

    P = 128
    N, D = x.shape
    RT = -(-N // P)
    NP = RT * P
    LAST = N - (RT - 1) * P
    KC = D // P
    S = w_sel_x.shape[2]
    G = 4
    SUB = D // P
    EC = src_main.shape[1]
    ET = src_tail.shape[0]
    NQ = 4
    ECP = -(-(EC + 1) // NQ) * NQ
    NN = NP * NP
    CW = NN // P + 1
    ITERS = 10
    COLS = [(c, min(512, NP - c)) for c in range(0, NP, 512)]
    TB = 250
    SG = S * G
    CHUNKS = (N // TB - 1) * SG
    TG = 25
    NBLK = N // TG
    EPS = 1e-5
    WARM = 5
    A, B = 11, 13
    MS, OS = 15, 11
    GATE_SCALE = float(2 ** (A + B + 1))
    WB = 4
    WIT = S * KC * 2 // WB

    adj = [nc.dram_tensor(f"adjacency_{b}", (P * CW,), f32, kind="Internal").ap() for b in range(2)]
    gx_dram = nc.dram_tensor("gate_inputs", (SG, P, N, SUB), f32, kind="Internal").ap()
    lx_dram = nc.dram_tensor("logit_inputs", (NP, S), f32, kind="Internal").ap()
    pick_dram = nc.dram_tensor("guessed_sets", (NP,), i32, kind="Internal").ap()
    x1_dram = nc.dram_tensor("x1_rows", (NP, D), f32, kind="Internal").ap()

    ctx = ExitStack()
    with ctx:
        def sb(name, shape, dt, where=ctx):
            return where.enter_context(nc.sbuf_tensor(name, shape, dt))

        def sem(name):
            return ctx.enter_context(nc.semaphore(name))

        ident = sb("ident", [P, P], f32)
        ones = sb("ones", [P, P], f32)
        xT = sb("xT", [P, KC, NP], f32)
        scal = sb("scal", [1, 3 + S], f32)
        scal_b = sb("scal_b", [P, 3 + S], f32)
        ab = sb("ab", [P, 4], f32)
        stats = sb("stats", [P, RT, 6], f32)
        mv = sb("mv", [P, RT, 2], f32)
        rstd = sb("rstd", [P, RT], f32)
        square = sb("square", [P, RT], f32)
        root = sb("root", [P, RT], f32)
        newton = sb("newton", [P, RT], f32)
        ramp = sb("ramp", [P, S], f32)
        biases = sb("biases", [P, S * G * SUB], f32)
        bias2 = sb("bias2", [P, S * G * SUB], f32)
        gscale = sb("gscale", [P, S * G * SUB], f32)
        wselx = sb("wselx", [P, KC, S], f32)
        wsel = sb("wsel", [P, S, 2 * SUB], f32)
        lx_t = sb("lx_t", [P, RT, S], f32)
        lx_w = sb("lx_w", [P, RT, S], f32)
        lx_m = sb("lx_m", [P, RT], f32)
        pick_t = sb("pick_t", [P, RT], i32)
        with ExitStack() as graph:
            X = sb("X", [P, RT, D], f32, graph)
            O0 = sb("O0", [P, RT, D], f32, graph)
            O1 = sb("O1", [P, RT, D], f32, graph)
            Adj = sb("Adj", [P, RT, NP], f32, graph)
            Adj1 = sb("Adj1", [P, CW], f32, graph)
            sim = sb("sim", [P, 2, NP], f32, graph)
            not_ident = sb("not_ident", [P, P], f32, graph)
            below = sb("below", [P, P], f32, graph)
            src_i = sb("src_i", [P, ECP], i32, graph)
            dst_i = sb("dst_i", [P, ECP], i32, graph)
            src_f = sb("src_f", [P, ECP], f32, graph)
            dst_f = sb("dst_f", [P, ECP], f32, graph)
            ew = sb("ew", [P, ECP], f32, graph)
            key = sb("key", [P, ECP], f32, graph)
            to_dump = sb("to_dump", [P, ECP], f32, graph)
            dump_i = sb("dump_i", [P, 1], i32, graph)
            dump_f = sb("dump_f", [P, 1], f32, graph)
            kdiag = sb("kdiag", [P, NQ, P], f32, graph)
            same = sb("same", [P, NQ, P], f32, graph)
            junk = sb("junk", [P, NQ, P], f32, graph)
            earlier = sb("earlier", [P, NQ], f32, graph)
            shift = sb("shift", [P, NQ], f32, graph)
            total = sb("total", [P, NQ, 1], f32, graph)
            where_ = sb("where_", [P, NQ, 1], u32, graph)
            sumsq = sb("sumsq", [P, RT], f32, graph)
            den = sb("den", [P, RT], f32, graph)
            adn = sb("adn", [P, RT], f32, graph)
            bdn = sb("bdn", [P, RT], f32, graph)
        M_parts = Adj1[:, 0:RT * NP].bitcast(f16).rearrange("p (a t n) -> p a t n", a=2, t=RT)
        O_parts = [o[:, :, :].bitcast(f16).rearrange("p t (a d) -> p a t d", a=2) for o in (O0, O1)]
        adj_words = Adj[:, :, :].rearrange("p t n -> p (t n)")
        XB = adj_words[:, 0:RT * D].rearrange("p (t d) -> p t d", t=RT)
        T = adj_words[:, RT * D:2 * RT * D].rearrange("p (t d) -> p t d", t=RT)
        inv_b = sim[:, 0, :]

        WH = sb("WH", [P, S * KC, 2, 4, D], f16)
        with ExitStack() as project:
            wst = sb("wst", [P, WB, 2, D], f32, project)
            wih = sb("wih", [P, G, KC, D], f32, project)
            gstage = sb("gstage", [P, 2, TB, SUB], f32, project)
        gateT = sb("gateT", [P, G * SUB, 33], f32)
        gates = sb("gates", [P, G * SUB], f32)
        acts = sb("acts", [P, G * SUB + SUB], f32)
        cprod = sb("cprod", [P, 2 * SUB], f32)
        osig = sb("osig", [P, SUB], f32)
        tanc = sb("tanc", [P, SUB], f32)
        hfull = sb("hfull", [P, SUB], f32)
        hparts = sb("hparts", [P, SUB, 17], f16)
        lprod = sb("lprod", [P, S, 2 * SUB + 1], f32)
        lpart = sb("lpart", [P, S], f32)
        lmax = sb("lmax", [1, 1], f32)
        lmark = sb("lmark", [1, S], f32)
        pick = sb("pick", [1, 1], i32)
        hist = xT
        gblk = sb("gblk", [P, 2, SG, TG, SUB], f32)
        wih_next = sb("wih_next", [P, SUB, KC, P], f32)
        gx_next = sb("gx_next", [P, 2, TB, SUB], f32)
        lx_row = sb("lx_row", [1, NP, S], f32)
        pick_row = sb("pick_row", [1, NP], i32)
        x1_t = wih_next[:, 0:2, :, :].rearrange("p b k n -> p b (k n)")
        out_t = wih_next[:, 2:4, :, :].rearrange("p b k n -> p b (k n)")

        ps = ctx.enter_context(nc.psum_tensor("ps", [P, 8, 512], f32))
        gate_ps = ps[:, 0, :]
        logit_ps = ps[0:1, 1, 0:S]
        seal_ps = ps[0:1, 2, 0:1]
        unit_ps = ps[:, 3, 0:TB]

        x_in = sem("x_in")
        square_ready = sem("square_ready")
        root_ready = sem("root_ready")
        edges_in = sem("edges_in")
        adj_zeroed = sem("adj_zeroed")
        places_free = [sem(f"places_free{b}") for b in range(NQ)]
        small_in = sem("small_in")
        zero_set = sem("zero_set")
        consts = sem("consts")
        masks = sem("masks")
        v = sem("v")
        a = sem("a")
        scal_mm = sem("scal_mm")
        ab_ready = sem("ab_ready")
        xn_ready = sem("xn_ready")
        trans_mm = sem("trans_mm")
        trans_out = sem("trans_out")
        edge_ready = sem("edge_ready")
        kd_ready = [sem(f"kd_ready{b}") for b in range(NQ)]
        kr_ready = [sem(f"kr_ready{b}") for b in range(NQ)]
        same_ready = [sem(f"same_ready{b}") for b in range(NQ)]
        earlier_ready = [sem(f"earlier_ready{b}") for b in range(NQ)]
        shift_ready = [sem(f"shift_ready{b}") for b in range(NQ)]
        total_mm = [sem(f"total_mm{b}") for b in range(NQ)]
        edge_out = [sem(f"edge_out{b}") for b in range(NQ)]
        places_ready = [sem(f"places_ready{b}") for b in range(NQ)]
        prop_ready = sem("prop_ready")
        scattered = [sem(f"scattered{b}") for b in range(2)]
        adj_in = sem("adj_in")
        adj_sum = sem("adj_sum")
        sim_mm = sem("sim_mm")
        sim_masked = sem("sim_masked")
        sim_exp = sem("sim_exp")
        adj_ready = sem("adj_ready")
        deg_mm = sem("deg_mm")
        prop_mm = sem("prop_mm")
        m_ready = sem("m_ready")
        m_high = sem("m_high")
        m_low = sem("m_low")
        t_ready = sem("t_ready")
        t_high = sem("t_high")
        t_low = sem("t_low")
        x1_ready = sem("x1_ready")
        x1_out = sem("x1_out")
        y_ready = sem("y_ready")
        lx_mm = sem("lx_mm")
        lx_ready = sem("lx_ready")
        lx_out = sem("lx_out")
        graph_free = sem("graph_free")
        wih_in = [sem(f"wih_in{g}") for g in range(G)]
        proj_mm = sem("proj_mm")
        proj_out = sem("proj_out")
        gx_stored = sem("gx_stored")
        whh_in = [sem(f"whh_in{b}") for b in range(WB)]
        whh_scaled = [sem(f"whh_scaled{b}") for b in range(WB)]
        whh_high = [sem(f"whh_high{b}") for b in range(WB)]
        whh_low = [sem(f"whh_low{b}") for b in range(WB)]
        wih_next_in = sem("wih_next_in")
        unit_mm = sem("unit_mm")
        unit_out = sem("unit_out")
        rows_in = sem("rows_in")
        gblk_in = [sem(f"gblk_in{b}") for b in range(2)]
        lx0_set = sem("lx0_set")
        lx_next = sem("lx_next")
        hist_free = sem("hist_free")
        h_ready = sem("h_ready")
        lpart_ready = sem("lpart_ready")
        logits_mm = sem("logits_mm")
        lmax_ready = sem("lmax_ready")
        lmark_ready = sem("lmark_ready")
        pick_ready = sem("pick_ready")
        scatter_seen = sem("scatter_seen")
        stage_seen = sem("stage_seen")
        pick_seen = sem("pick_seen")
        gates_mm = sem("gates_mm")
        turned = sem("turned")
        gx_set = sem("gx_set")
        gates_ready = sem("gates_ready")
        acts_ready = sem("acts_ready")
        cprod_ready = sem("cprod_ready")
        osig_ready = sem("osig_ready")
        c_ready = sem("c_ready")
        tanc_ready = sem("tanc_ready")
        h_full = sem("h_full")
        lprod_c = sem("lprod_c")
        lprod_h = sem("lprod_h")
        x1_back = [sem(f"x1_back{b}") for b in range(2)]
        out_mm = sem("out_mm")
        out_sum = sem("out_sum")
        out_done = [sem(f"out_done{b}") for b in range(2)]

        EIT = ECP // NQ
        NCH = len(COLS)
        TQ = [(q, min(4, RT - q)) for q in range(0, RT, 4)]
        NTQ = KC * len(TQ)

        block = ctx.enter_context(nc.Block())

        @block.sync
        def _(sp):
            sp.wait_ge(zero_set, 1)
            sp.dma_start(X[:, 0:RT - 1, :], x[0:(RT - 1) * P, :].rearrange("(t p) d -> p t d", p=P)).then_inc(x_in, 16)
            sp.dma_start(X[0:LAST, RT - 1, :], x[(RT - 1) * P:N, :]).then_inc(x_in, 16)
            sp.wait_ge(zero_set, 2)
            for b in range(2):
                sp.dma_start(adj[b].rearrange("(p n) -> p n", p=P), Adj1[:, :]).then_inc(adj_zeroed, 16)
            for b in range(2):
                sp.wait_ge(scattered[b], 16 * EIT * (NQ // 2))
            sp.dma_start(Adj[:, :, :], adj[0][0:NN].rearrange("(t p n) -> p t n", p=P, n=NP)).then_inc(adj_in, 16)
            sp.dma_start(Adj1[:, 0:RT * NP].rearrange("p (t n) -> p t n", t=RT),
                         adj[1][0:NN].rearrange("(t p n) -> p t n", p=P, n=NP)).then_inc(adj_in, 16)
            sp.wait_ge(x1_ready, 1)
            sp.dma_start(x1_dram.rearrange("(t p) d -> p t d", p=P), X[:, :, :]).then_inc(x1_out, 16)
            sp.wait_ge(lx_ready, 1)
            sp.dma_start(lx_dram.rearrange("(t p) s -> p t s", p=P), lx_t[:, :, :]).then_inc(lx_out, 16)
            sp.dma_start(pick_dram.rearrange("(t p) -> p t", p=P), pick_t[:, :], allow_slow_non_contiguous=True).then_inc(lx_out, 16)
            sp.wait_ge(x1_out, 16)
            sp.wait_ge(graph_free, 1)
            for g in range(G):
                sp.dma_start(wih[:, g, :, :].rearrange("p k n -> p (k n)"), w_ih[:, 0, g, :]).then_inc(wih_in[g], 16)

            def store(s, g):
                taken = sp.snap(s * (G * SUB) + (g * SUB + SUB + 8))
                landed = sp.snap(s * (16 * G) + (16 * g + 32))
                chunk = sp.snap(s * G + g)
                sp.wait_ge(proj_out, taken)
                sp.sem_inc(stage_seen, 1)
                sp.wait_ge(gx_stored, landed)
                sp.dma_start(gx_dram[bass.ds(chunk, 1), :, 0:TB, :].rearrange("a p t c -> p (a t c)"),
                             gstage[:, g % 2, :, :].rearrange("p t c -> p (t c)")).then_inc(gx_stored, 16)

            with sp.Fori(0, S - 1) as s:
                for g in range(G):
                    sp.wait_ge(proj_mm, sp.snap(s * (G * SUB) + (g + 1) * SUB))
                    sp.dma_start(wih[:, g, :, :].rearrange("p k n -> p (k n)"),
                                 w_ih[:, bass.ds(s + 1, 1), g, :].rearrange("p a n -> p (a n)")).then_inc(wih_in[g], 16)
                    store(s, g)
            for g in range(G):
                store(sp.snap(S - 1), g)
            sp.wait_ge(gx_stored, 16 * (SG + 2))
            sp.wait_ge(lx_out, 32)
            for b in range(WB):
                sp.wait_ge(whh_low[b], WIT + 1)
            sp.dma_start(lx_row[0:1, :, :], lx_dram.rearrange("(a t) s -> a t s", a=1)).then_inc(rows_in, 16)
            sp.dma_start(pick_row[0:1, :], pick_dram.rearrange("(a t) -> a t", a=1)).then_inc(rows_in, 16)
            for b in range(2):
                sp.dma_start(gblk[:, b, :, :, :].rearrange("p s t c -> p s (t c)"),
                             gx_dram[:, :, b * TG:(b + 1) * TG, :].rearrange("s p t c -> p s (t c)")).then_inc(gblk_in[b], 16)
            w_units = w_ih.rearrange("p s g (k u n) -> p (s g) k u n", k=KC, u=SUB)

            def load_unit(c, u):
                sp.dma_start(wih_next[:, bass.ds(u, 1), :, :].rearrange("p a k n -> p (a k) n"),
                             w_units[:, bass.ds(c % SG, 1), :, bass.ds(u, 1), :].rearrange("p a k u n -> p (a k) (u n)")
                             ).then_inc(wih_next_in, 16)

            def store_chunk(c):
                sp.wait_ge(unit_out, sp.snap(c * SUB + (SUB + 1)))
                sp.wait_ge(gx_stored, sp.snap(c * 16 + 16 * (SG + 2)))
                sp.dma_start(gx_dram[bass.ds(c % SG, 1), :, bass.ds((c // SG) * TB + TB, TB), :].rearrange("a p t c -> p (a t c)"),
                             gx_next[:, bass.ds(c % 2, 1), :, :].rearrange("p a t c -> p (a t c)")).then_inc(gx_stored, 16)

            for u in range(SUB):
                load_unit(sp.snap(0), u)
                sp.wait_ge(wih_next_in, 16 * (u + 1))
            with sp.Fori(0, CHUNKS - 1) as c:
                with sp.Fori(0, SUB) as u:
                    t = sp.snap(c * SUB + u)
                    sp.wait_ge(unit_mm, sp.snap(t + 1))
                    sp.wait_ge(wih_next_in, sp.snap(t * 16 + 16 * SUB))
                    load_unit(sp.snap(c + 1), u)
                store_chunk(c)
            store_chunk(sp.snap(CHUNKS - 1))
            sp.wait_ge(unit_mm, CHUNKS * SUB)
            sp.wait_ge(wih_next_in, 16 * CHUNKS * SUB)
            sp.wait_ge(gx_stored, 16 * (SG + 2 + CHUNKS))
            for t in range(RT):
                b = t % 2
                if t >= 2:
                    sp.wait_ge(out_sum, SUB * (t - 1))
                sp.dma_start(x1_t[:, b, :], x1_dram[t * P:(t + 1) * P, :]).then_inc(x1_back[b], 16)
            for b in range(2):
                sp.wait_ge(out_done[b], 16 * (RT // 2))

        @block.gpsimd
        def _(pool):
            pool.wait_ge(consts, 1)
            pool.affine_select(out=below[:, :], in_=ones[:, :], compare_op=ALU.is_gt, fill=0.0, base=0,
                               pattern=[[-1, P]], channel_multiplier=1).then_inc(masks, 1)
            pool.affine_select(out=not_ident[:, :], in_=ones[:, :], compare_op=ALU.not_equal, fill=0.0, base=0,
                               pattern=[[-1, P]], channel_multiplier=1).then_inc(masks, 1)
            pool.wait_ge(consts, 2)
            pool.affine_select(out=ident[:, :], in_=ident[:, :], compare_op=ALU.not_equal, fill=1.0, base=0,
                               pattern=[[-1, P]], channel_multiplier=1).then_inc(masks, 1)
            pool.iota(dump_i[:, :], pattern=[[0, 1]], base=NN, channel_multiplier=1).then_inc(masks, 1)
            last_word = pool.alloc_register("last_word")
            pool.reg_mov(last_word, P * CW - 1)
            pool.wait_ge(adj_zeroed, 32)
            for q in range(NQ):
                pool.sem_inc(places_free[q], 1)

            def scatter(q, n):
                pool.wait_ge(places_ready[q], n)
                pool.wait_ge(edge_out[q], n)
                pool.sem_inc(scatter_seen, 1)
                pool.indirect_dma_start(
                    out=adj[q % 2].rearrange("(n a) -> n a", a=1),
                    out_offset=bass.IndirectOffsetOnAxis(ap=where_[:, q, :], axis=0),
                    in_=total[:, q, :], in_offset=None, compute_op=ALU.add,
                    bounds_check=last_word, oob_is_err=True).then_inc(scattered[q % 2], 16)

            def landed(q, n16):
                pool.wait_ge(scattered[q % 2], n16)
                pool.sem_inc(places_free[q], 1)

            scatter(0, 1)
            scatter(1, 1)
            landed(0, 16)
            scatter(2, 1)
            landed(1, 16)
            scatter(3, 1)
            landed(2, 32)
            with pool.Fori(1, EIT) as i:
                n = pool.snap(i + 1)
                before = pool.snap(i * 32)
                first = pool.snap(i * 32 + 16)
                second = pool.snap(i * 32 + 32)
                scatter(0, n)
                landed(3, before)
                scatter(1, n)
                landed(0, first)
                scatter(2, n)
                landed(1, first)
                scatter(3, n)
                landed(2, second)
            landed(3, 32 * EIT)
            for r in range(RT):
                pool.wait_ge(m_high, r + 1)
                pool.tensor_tensor(M_parts[:, 1, r, :], Adj[:, r, :], M_parts[:, 0, r, :], ALU.subtract).then_inc(m_low, 1)

            def low_part(new, r, n):
                pool.wait_ge(t_high, n)
                pool.tensor_tensor(new[:, 1, r, :], T[:, r, :], new[:, 0, r, :], ALU.subtract).then_inc(t_low, 1)

            for r in range(RT):
                low_part(O_parts[1], r, r + 1)
            with pool.Fori(0, ITERS // 2) as i:
                for half in range(2):
                    for r in range(RT):
                        low_part(O_parts[half], r, pool.snap(i * (2 * RT) + (RT + half * RT + r + 1)))
            for b in range(WB):
                pool.sem_inc(whh_low[b], 1)
            with pool.Fori(0, WIT) as i:
                n = pool.snap(i + 1)
                for b in range(WB):
                    j = 2 * (b % 2)
                    chunk = bass.ds(i * (WB // 2) + b // 2, 1)
                    pool.wait_ge(whh_high[b], n)
                    pool.tensor_tensor(WH[:, chunk, 1, j:j + 2, :].rearrange("p a j n -> p (a j n)"),
                                       wst[:, b, :, :].rearrange("p j n -> p (j n)"),
                                       WH[:, chunk, 0, j:j + 2, :].rearrange("p a j n -> p (a j n)"),
                                       ALU.subtract).then_inc(whh_low[b], 1)
            pool.wait_ge(rows_in, 32)
            pool.wait_ge(lx_ready, 2)
            pool.tensor_copy(lprod[0:1, :, 2 * SUB], lx_row[0:1, 0, :]).then_inc(lx0_set, 1)

            def side_steps(t, n, n2):
                pool.wait_ge(lpart_ready, n)
                pool.tensor_copy(lprod[0:1, :, 2 * SUB:2 * SUB + 1].rearrange("a s c -> a (s c)"),
                                 lx_row[0:1, bass.ds(t + 1, 1), :].rearrange("a t s -> a (t s)")).then_inc(lx_next, 1)
                pool.wait_ge(h_full, n2)
                pool.tensor_copy(hist[:, :, bass.ds(t, 1)].rearrange("p s t -> p (s t)"), hfull[:, :]).then_inc(hist_free, 1)

            with pool.Fori(0, N) as t:
                side_steps(t, pool.snap(t + 1), pool.snap(t * 2 + 2))

        @block.scalar
        def _(act):
            chain = [0]

            def link(ins):
                chain[0] += 1
                ins.then_inc(a, 1)
                act.wait_ge(a, chain[0])

            act.dma_start(scal[:, :], scalars).then_inc(small_in, 16)
            act.dma_start(biases[:, :], b_ih).then_inc(small_in, 16)
            act.dma_start(bias2[:, :], b_hh).then_inc(small_in, 16)
            act.dma_start(wselx[:, :, :], w_sel_x).then_inc(small_in, 16)
            act.dma_start(wsel[:, :, :], w_sel_state).then_inc(small_in, 16)
            act.wait_ge(edge_ready, 1)
            for tile, main, tail in ((src_i, src_main, src_tail), (dst_i, dst_main, dst_tail), (ew, ew_main, ew_tail)):
                act.dma_start(tile[:, 0:EC], main).then_inc(edges_in, 16)
                act.dma_start(tile[0:ET, EC:EC + 1], tail).then_inc(edges_in, 16)
            act.wait_ge(scal_mm, 2)
            act.activation(ab[:, 0:2], scal_b[:, 0:2], ACT.Exp).then_inc(ab_ready, 1)
            act.activation(ab[:, 2:3], scal_b[:, 2:3], ACT.Exp, scale=-2.0).then_inc(ab_ready, 1)

            def take_root(n):
                act.wait_ge(square_ready, n)
                act.activation(root[:, :], square[:, :], ACT.Sqrt).then_inc(root_ready, 1)

            take_root(1)
            take_root(2)

            def evacuate_transposes(first):
                for k in range(KC):
                    for q, (r0, m) in enumerate(TQ):
                        i = first + k * len(TQ) + q
                        act.wait_ge(trans_mm, i + 1)
                        act.activation(xT[:, k, r0 * P:(r0 + m) * P], ps[:, i % 8, 0:m * P], ACT.Copy).then_inc(trans_out, 1)

            evacuate_transposes(0)
            act.wait_ge(ab_ready, 3)
            for r in range(RT):
                for c, (c0, m) in enumerate(COLS):
                    act.wait_ge(sim_mm, NCH * r + c + 1)
                    if c0 <= r * P < c0 + m:
                        act.wait_ge(sim_masked, r + 1)
                    if r >= 2:
                        act.wait_ge(adj_ready, r - 1)
                    act.activation(sim[:, r % 2, c0:c0 + m], ps[:, 2 + 3 * (r % 2) + c, 0:m], ACT.Exp,
                                   scale=ab[:, 3:4]).then_inc(sim_exp, 1)
            for r in range(RT):
                act.wait_ge(m_ready, r + 1)
                act.activation(M_parts[:, 0, r, :], Adj[:, r, :], ACT.Copy).then_inc(m_high, 1)

            def high_part(new, r, n):
                act.wait_ge(t_ready, n)
                act.activation(new[:, 0, r, :], T[:, r, :], ACT.Copy).then_inc(t_high, 1)

            for r in range(RT):
                high_part(O_parts[1], r, r + 1)
            with act.Fori(0, ITERS // 2) as i:
                for half in range(2):
                    for r in range(RT):
                        high_part(O_parts[half], r, act.snap(i * (2 * RT) + (RT + half * RT + r + 1)))
            take_root(3)
            evacuate_transposes(NTQ)
            act.wait_ge(x1_out, 16)
            act.wait_ge(graph_free, 1)
            w_v = w_hh.rearrange("p (c b n) -> p c b n", c=S * KC, b=2)

            def load_half(i, b):
                act.wait_ge(whh_low[b], act.snap(i + 1))
                act.dma_start(wst[:, b, :, :].rearrange("p j n -> p (j n)"),
                              w_v[:, bass.ds(i * (WB // 2) + b // 2, 1), b % 2, :].rearrange("p a n -> p (a n)")).then_inc(whh_in[b], 16)

            def split_halves(i, more):
                for b in range(WB):
                    j = 2 * (b % 2)
                    if b + 2 < WB:
                        load_half(i, b + 2)
                    elif more:
                        load_half(act.snap(i + 1), b + 2 - WB)
                    act.wait_ge(whh_in[b], act.snap(i * 16 + 16))
                    act.activation(wst[:, b, :, 0:3 * P], wst[:, b, :, 0:3 * P], ACT.Copy, scale=float(2 ** (A - 1))).then_inc(whh_scaled[b], 1)
                    act.activation(wst[:, b, :, 3 * P:D], wst[:, b, :, 3 * P:D], ACT.Copy, scale=float(2 ** A)).then_inc(whh_scaled[b], 1)
                    act.wait_ge(whh_scaled[b], act.snap(i * 2 + 2))
                    act.activation(WH[:, bass.ds(i * (WB // 2) + b // 2, 1), 0, j:j + 2, :].rearrange("p a j n -> p (a j n)"),
                                   wst[:, b, :, :].rearrange("p j n -> p (j n)"), ACT.Copy).then_inc(whh_high[b], 1)

            for b in range(2):
                load_half(act.snap(0), b)
            with act.Fori(0, WIT - 1) as i:
                split_halves(i, True)
            split_halves(act.snap(WIT - 1), False)
            act.activation(root[:, :], square[:, :], ACT.Tanh)
            def act_block(i, b, stored):
                act.wait_ge(gblk_in[b], act.snap(i * 16 + 16))
                with act.Fori(0, TG) as tl:
                    n = act.snap(i * (2 * TG) + tl + (b * TG + 1))
                    act.wait_ge(pick_ready, n)
                    act.sem_inc(pick_seen, 1)
                    r = act.value_load(pick[0:1, 0:1], min_val=1, max_val=S)
                    act.activation(gateT[:, :, 32:33].rearrange("p (g c) a -> p g (c a)", g=G),
                                   gblk[:, b, bass.ds(r * G - G, G), bass.ds(tl, 1), :].rearrange("p s t c -> p s (t c)"),
                                   ACT.Copy).then_inc(gx_set, 1)
                    act.wait_ge(gates_ready, n)
                    act.activation(acts[:, 0:G * SUB], gates[:, :], ACT.Tanh, scale=1.0 / GATE_SCALE).then_inc(acts_ready, 1)
                    act.wait_ge(c_ready, n)
                    act.activation(tanc[:, :], acts[:, G * SUB:G * SUB + SUB], ACT.Tanh, scale=0.5).then_inc(tanc_ready, 1)
                if stored is not None:
                    act.wait_ge(gx_set, act.snap(i * (2 * TG) + (b + 1) * TG))
                    act.wait_ge(gx_stored, stored)
                    act.dma_start(gblk[:, b, :, :, :].rearrange("p s t c -> p s (t c)"),
                                  gx_dram[:, :, bass.ds(i * (2 * TG) + (b + 2) * TG, TG), :].rearrange("s p t c -> p s (t c)")
                                  ).then_inc(gblk_in[b], 16)

            ahead = -(-CHUNKS * SUB // (2 * TG)) - 1
            with act.Fori(0, ahead) as i:
                stored = act.snap(i * (16 * SG // (TB // (2 * TG) - 1)) + 16 * (SG + 2))
                for b in range(2):
                    act_block(i, b, stored)
            with act.Fori(ahead, NBLK // 2 - 1) as i:
                for b in range(2):
                    act_block(i, b, 16 * (SG + 2 + CHUNKS))
            for b in range(2):
                act_block(act.snap(NBLK // 2 - 1), b, None)
            for t in range(RT):
                b = t % 2
                rows = P if t < RT - 1 else LAST
                act.wait_ge(out_sum, SUB * (t + 1))
                act.dma_start(out[t * P:t * P + rows, :], out_t[0:rows, b, :]).then_inc(out_done[b], 16)

        @block.vector
        def _(dve):
            chain = [0]

            def link(ins):
                chain[0] += 1
                ins.then_inc(v, 1)
                dve.wait_ge(v, chain[0])

            dve.memset(X[:, RT - 1, :], 0.0).then_inc(zero_set, 1)
            dve.memset(Adj1[:, :], 0.0).then_inc(zero_set, 1)
            dve.memset(ones[:, :], 1.0).then_inc(consts, 1)
            dve.memset(ident[:, :], 0.0).then_inc(consts, 1)
            dve.memset(src_i[:, :], 0)
            dve.memset(dst_i[:, :], 0)
            dve.memset(ew[:, :], 0.0).then_inc(edge_ready, 1)
            for s in range(S):
                link(dve.memset(ramp[:, s:s + 1], float(S - s)))

            dve.wait_ge(scal_mm, 1)
            dve.tensor_copy(scal_b[:, :], ps[:, 7, 0:3 + S]).then_inc(scal_mm, 1)
            dve.wait_ge(ab_ready, 2)
            dve.tensor_scalar(ab[:, 3:4], ab[:, 2:3], 0.25, None, ALU.mult).then_inc(ab_ready, 1)

            roots = [0]

            def inverse_root(to):
                roots[0] += 1
                dve.sem_inc(square_ready, 1)
                dve.wait_ge(root_ready, roots[0])
                link(dve.reciprocal(to[:, :], root[:, :]))
                link(dve.tensor_tensor(newton[:, :], to[:, :], to[:, :], ALU.mult))
                link(dve.tensor_tensor(newton[:, :], newton[:, :], square[:, :], ALU.mult))
                link(dve.tensor_scalar(newton[:, :], newton[:, :], -0.5, 1.5, ALU.mult, ALU.add))
                link(dve.tensor_tensor(to[:, :], to[:, :], newton[:, :], ALU.mult))

            def layernorm_stats():
                for r in range(RT):
                    dve.bn_stats(stats[:, r, :], X[:, r, :]).then_inc(v, 1)
                    chain[0] += 1
                dve.wait_ge(v, chain[0])
                for r in range(RT):
                    dve.bn_aggr(mv[:, r, :], stats[:, r, :]).then_inc(v, 1)
                    chain[0] += 1
                dve.wait_ge(v, chain[0])
                link(dve.tensor_scalar(square[:, :], mv[:, :, 1], EPS, None, ALU.add))
                inverse_root(rstd)

            dve.wait_ge(x_in, 32)
            layernorm_stats()
            for r in range(RT):
                link(dve.tensor_scalar(O0[:, r, :], X[:, r, :], mv[:, r, 0:1], rstd[:, r:r + 1], ALU.subtract, ALU.mult))
                link(dve.scalar_tensor_tensor(out=O1[:, r, :], in0=O0[:, r, :], scalar=1.0, in1=O0[:, r, :],
                                              op0=ALU.mult, op1=ALU.mult, accum_out=sumsq[:, r:r + 1]))
            link(dve.tensor_scalar(square[:, :], sumsq[:, :], 1e-12, None, ALU.max))
            inverse_root(sumsq)
            for r in range(RT):
                dve.tensor_scalar(O1[:, r, :], O0[:, r, :], sumsq[:, r:r + 1], None, ALU.mult).then_inc(xn_ready, 1)

            dve.wait_ge(masks, 4)
            link(dve.tensor_copy(dump_f[:, :], dump_i[:, :]))
            dve.wait_ge(edges_in, 16 * 6)
            link(dve.tensor_copy(src_f[:, :], src_i[:, :]))
            link(dve.tensor_copy(dst_f[:, :], dst_i[:, :]))
            for c in range(EC, ECP):
                link(dve.tensor_copy(key[:, c:c + 1], dump_f[:, :]))
            link(dve.scalar_tensor_tensor(out=key[:, 0:EC], in0=dst_f[:, 0:EC], scalar=float(NP), in1=src_f[:, 0:EC],
                                          op0=ALU.mult, op1=ALU.add))
            link(dve.scalar_tensor_tensor(out=key[0:ET, EC:EC + 1], in0=dst_f[0:ET, EC:EC + 1], scalar=float(NP),
                                          in1=src_f[0:ET, EC:EC + 1], op0=ALU.mult, op1=ALU.add))
            link(dve.tensor_scalar(to_dump[:, :], key[:, :], dump_f[:, 0:1], -1.0, ALU.subtract, ALU.mult))
            with dve.Fori(0, EIT) as i:
                n = dve.snap(i + 1)
                kcol = [key[:, bass.ds(i * NQ + b, 1)] for b in range(NQ)]
                dcol = [to_dump[:, bass.ds(i * NQ + b, 1)] for b in range(NQ)]
                for b in range(NQ):
                    dve.tensor_scalar(kdiag[:, b, :], ident[:, :], kcol[b], None, ALU.mult).then_inc(kd_ready[b], 1)
                for b in range(NQ):
                    dve.wait_ge(kr_ready[b], n)
                    dve.tensor_scalar(same[:, b, :], ps[:, 2 * b, 0:P], kcol[b], None, ALU.is_equal).then_inc(same_ready[b], 1)
                    dve.scalar_tensor_tensor(out=junk[:, b, :], in0=ps[:, 2 * b, 0:P], scalar=kcol[b], in1=below[:, :],
                                             op0=ALU.is_equal, op1=ALU.mult, accum_out=earlier[:, b:b + 1]).then_inc(earlier_ready[b], 1)
                for b in range(NQ):
                    dve.wait_ge(earlier_ready[b], n)
                    dve.scalar_tensor_tensor(out=shift[:, b:b + 1], in0=earlier[:, b:b + 1], scalar=1.0, in1=dcol[b],
                                             op0=ALU.min, op1=ALU.mult).then_inc(shift_ready[b], 1)
                for b in range(NQ):
                    dve.wait_ge(shift_ready[b], n)
                    dve.wait_ge(places_free[b], n)
                    dve.tensor_tensor(where_[:, b, :], shift[:, b:b + 1], kcol[b], ALU.add).then_inc(places_ready[b], 1)
                    dve.wait_ge(total_mm[b], n)
                    dve.tensor_copy(total[:, b, :], ps[:, 2 * b + 1, 0:1]).then_inc(edge_out[b], 1)
            dve.wait_ge(adj_in, 32)
            for r in range(RT):
                dve.tensor_tensor(Adj[:, r, :], Adj[:, r, :], Adj1[:, r * NP:(r + 1) * NP], ALU.add).then_inc(adj_sum, 1)
            for r in range(RT):
                c = r // 4
                q = r * P - COLS[c][0]
                dve.wait_ge(sim_mm, NCH * r + c + 1)
                blk = ps[:, 2 + 3 * (r % 2) + c, q:q + P]
                dve.tensor_tensor(blk, blk, not_ident[:, :], ALU.mult).then_inc(sim_masked, 1)
                dve.wait_ge(adj_sum, r + 1)
                dve.wait_ge(sim_exp, NCH * (r + 1))
                dve.tensor_tensor(Adj[:, r, :], Adj[:, r, :], sim[:, r % 2, :], ALU.mult).then_inc(adj_ready, 1)
            dve.wait_ge(deg_mm, 1)
            for c, (c0, m) in enumerate(COLS):
                link(dve.tensor_scalar(inv_b[:, c0:c0 + m], ps[:, c, 0:m], ab[:, 0:1], ab[:, 1:2], ALU.mult, ALU.add))
            link(dve.tensor_scalar(inv_b, inv_b, ab[:, 0:1], None, ALU.add))
            link(dve.reciprocal(inv_b, inv_b))
            for r in range(RT):
                link(dve.scalar_tensor_tensor(out=junk[:, 0, :], in0=inv_b[:, r * P:(r + 1) * P], scalar=1.0, in1=ident[:, :],
                                              op0=ALU.mult, op1=ALU.mult, accum_out=den[:, r:r + 1]))
            link(dve.tensor_scalar(adn[:, :], den[:, :], ab[:, 0:1], float(2 ** MS), ALU.mult, ALU.mult))
            link(dve.tensor_scalar(bdn[:, :], den[:, :], ab[:, 1:2], float(2 ** OS), ALU.mult, ALU.mult))
            link(dve.tensor_scalar(inv_b, inv_b, ab[:, 0:1], float(2 ** MS), ALU.mult, ALU.mult))
            for r in range(RT):
                link(dve.tensor_tensor(Adj[:, r, :], Adj[:, r, :], inv_b, ALU.mult))
                blk = Adj[:, r, r * P:(r + 1) * P]
                dve.scalar_tensor_tensor(out=blk, in0=ident[:, :], scalar=adn[:, r:r + 1], in1=blk,
                                         op0=ALU.mult, op1=ALU.add).then_inc(m_ready, 1)
            dve.wait_ge(m_low, RT)
            for r in range(RT):
                dve.tensor_scalar(T[:, r, :], O0[:, r, :], float(2 ** OS), None, ALU.mult).then_inc(t_ready, 1)
            for r in range(RT):
                link(dve.tensor_scalar(XB[:, r, :], O0[:, r, :], bdn[:, r:r + 1], None, ALU.mult))
            dve.sem_inc(prop_ready, 1)
            with dve.Fori(0, ITERS // 2) as i:
                for half in range(2):
                    for r in range(RT):
                        dve.wait_ge(prop_mm, dve.snap(i * (2 * RT) + (half * RT + r + 1)))
                        dve.scalar_tensor_tensor(out=T[:, r, :], in0=ps[:, r % 8, :], scalar=float(2.0 ** -MS), in1=XB[:, r, :],
                                                 op0=ALU.mult, op1=ALU.add).then_inc(t_ready, 1)
            dve.wait_ge(t_ready, (ITERS + 1) * RT)
            for r in range(RT):
                link(dve.scalar_tensor_tensor(out=X[:, r, :], in0=T[:, r, :], scalar=float(2.0 ** -OS), in1=X[:, r, :],
                                              op0=ALU.mult, op1=ALU.add))
            dve.sem_inc(x1_ready, 1)
            layernorm_stats()
            dve.wait_ge(t_low, (ITERS + 1) * RT)
            for r in range(RT):
                dve.tensor_scalar(O1[:, r, :], X[:, r, :], mv[:, r, 0:1], rstd[:, r:r + 1], ALU.subtract, ALU.mult).then_inc(y_ready, 1)
            dve.wait_ge(small_in, 16 * 5)
            dve.wait_ge(lx_mm, 1)
            bsel = scal_b[:, 3:3 + S].rearrange("p (a s) -> p a s", a=1).broadcast_to([P, RT, S])
            link(dve.tensor_tensor(lx_t[:, :, :], ps[:, 0, 0:RT * S].rearrange("p (t s) -> p t s", s=S), bsel, ALU.add))
            link(dve.memset(lx_t[0:1, 0, :], 0.0))
            link(dve.memset(lx_t[0:1, 0, 0:1], 1.0))
            link(dve.tensor_reduce(lx_m[:, :], lx_t[:, :, :], AX.X, ALU.max))
            link(dve.tensor_tensor(lx_w[:, :, :], lx_t[:, :, :], lx_m[:, :].rearrange("p (t a) -> p t a", a=1).broadcast_to([P, RT, S]), ALU.is_ge))
            link(dve.tensor_tensor(lx_w[:, :, :], lx_w[:, :, :], ramp[:, :].rearrange("p (a s) -> p a s", a=1).broadcast_to([P, RT, S]), ALU.mult))
            dve.tensor_reduce(pick_t[:, :], lx_w[:, :, :], AX.X, ALU.max).then_inc(lx_ready, 1)
            link(dve.tensor_tensor(biases[:, :], biases[:, :], bias2[:, :], ALU.add))
            bv = biases[:, :].rearrange("p (s g c) -> p s g c", s=S, g=G)
            link(dve.tensor_scalar(bv[:, :, 0:3, :], bv[:, :, 0:3, :], GATE_SCALE / 2, None, ALU.mult))
            link(dve.tensor_scalar(bv[:, :, 3:4, :], bv[:, :, 3:4, :], GATE_SCALE, None, ALU.mult))
            link(dve.tensor_scalar(wsel[:, :, 0:SUB], wsel[:, :, 0:SUB], 0.5, None, ALU.mult))
            link(dve.tensor_scalar(wsel[:, :, SUB:2 * SUB], wsel[:, :, SUB:2 * SUB], float(2.0 ** -(B + 1)), None, ALU.mult))
            gv = gscale[:, :].rearrange("p (s g c) -> p s g c", s=S, g=G)
            link(dve.memset(gv[:, :, 0:3, :], GATE_SCALE / 2))
            link(dve.memset(gv[:, :, 3:4, :], GATE_SCALE))
            dve.wait_ge(graph_free, 1)
            dve.wait_ge(x1_out, 16)
            dve.sem_inc(proj_out, 8)
            dve.sem_inc(gx_stored, 32)
            with dve.Fori(0, S) as s:
                for c in range(G * SUB):
                    if c % SUB == 0:
                        dve.wait_ge(gx_stored, dve.snap(s * (16 * G) + 16 * (c // SUB + 1)))
                    dve.wait_ge(proj_mm, dve.snap(s * (G * SUB) + (c + 1)))
                    dve.tensor_scalar(gstage[:, c // SUB % 2, :, c % SUB], ps[:, c % 8, 0:TB], GATE_SCALE if c // SUB == 3 else GATE_SCALE / 2,
                                      biases[:, bass.ds(s * (G * SUB) + c, 1)], ALU.mult, ALU.add).then_inc(proj_out, 1)
            for b in range(WB):
                dve.wait_ge(whh_low[b], WIT + 1)
            dve.wait_ge(gx_stored, 16 * (SG + 2))
            dve.wait_ge(proj_mm, S * G * SUB)
            dve.wait_ge(proj_out, S * G * SUB + 8)
            link(dve.memset(gateT[:, :, :], 0.0))
            link(dve.memset(gate_ps, 0.0))
            link(dve.memset(acts[:, G * SUB:G * SUB + SUB], 0.0))
            link(dve.memset(lprod[:, :, :], 0.0))
            dve.sem_inc(lx_ready, 1)
            dve.memset(hparts[:, :, :], 0.0).then_inc(h_ready, 1)
            dve.sem_inc(hist_free, 1)
            dve.wait_ge(lx0_set, 1)
            dve.tensor_reduce(lpart[:, :], lprod[:, :, :], AX.X, ALU.add).then_inc(lpart_ready, 1)

            def choose(n):
                dve.wait_ge(logits_mm, n)
                dve.tensor_reduce(lmax[:, :], logit_ps, AX.X, ALU.max).then_inc(lmax_ready, 1)
                dve.wait_ge(lmax_ready, n)
                dve.scalar_tensor_tensor(out=lmark[:, :], in0=logit_ps, scalar=lmax[:, 0:1], in1=ramp[0:1, :],
                                         op0=ALU.is_ge, op1=ALU.mult).then_inc(lmark_ready, 1)
                dve.wait_ge(lmark_ready, n)
                dve.tensor_reduce(pick[:, :], lmark[:, :], AX.X, ALU.max).then_inc(pick_ready, 1)

            def cell(n, n2):
                dve.wait_ge(gates_mm, n)
                dve.transpose(gateT[:, :, 0:32], gate_ps.rearrange("p (c q) -> p c q", q=32)).then_inc(turned, 1)
                dve.wait_ge(turned, n)
                dve.wait_ge(gx_set, n)
                dve.tensor_reduce(gates[:, :], gateT[:, :, 0:33:16], AX.X, ALU.add).then_inc(gates_ready, 1)
                dve.wait_ge(acts_ready, n)
                dve.scalar_tensor_tensor(out=cprod[:, :], in0=acts[:, 0:2 * SUB], scalar=1.0, in1=acts[:, 3 * SUB:5 * SUB],
                                         op0=ALU.add, op1=ALU.mult).then_inc(cprod_ready, 1)
                dve.tensor_scalar(osig[:, :], acts[:, 2 * SUB:3 * SUB], 1.0, float(2 ** B), ALU.add, ALU.mult).then_inc(osig_ready, 1)
                dve.wait_ge(cprod_ready, n)
                dve.scalar_tensor_tensor(out=acts[:, 4 * SUB:5 * SUB], in0=cprod[:, SUB:2 * SUB], scalar=0.5, in1=cprod[:, 0:SUB],
                                         op0=ALU.mult, op1=ALU.add).then_inc(c_ready, 1)
                dve.wait_ge(osig_ready, n)
                dve.wait_ge(lx_next, n)
                dve.wait_ge(hist_free, n)
                dve.wait_ge(c_ready, n)
                dve.tensor_tensor(lprod[:, :, 0:SUB], acts[:, 4 * SUB:5 * SUB].rearrange("p (a c) -> p a c", a=1).broadcast_to([P, S, SUB]),
                                  wsel[:, :, 0:SUB], ALU.mult).then_inc(lprod_c, 1)
                dve.wait_ge(tanc_ready, n)
                dve.tensor_tensor(hfull[:, :], osig[:, :], tanc[:, :], ALU.mult).then_inc(h_full, 1)
                dve.tensor_tensor(hparts[:, :, 0], osig[:, :], tanc[:, :], ALU.mult).then_inc(h_full, 1)
                dve.wait_ge(h_full, n2)
                dve.tensor_tensor(hparts[:, :, 16], hfull[:, :], hparts[:, :, 0], ALU.subtract).then_inc(h_ready, 1)

            def logit_parts(n):
                dve.wait_ge(lprod_c, n)
                dve.tensor_tensor(lprod[:, :, SUB:2 * SUB], hfull[:, :].rearrange("p (a c) -> p a c", a=1).broadcast_to([P, S, SUB]),
                                  wsel[:, :, SUB:2 * SUB], ALU.mult).then_inc(lprod_h, 1)
                dve.wait_ge(lprod_h, n)
                dve.tensor_reduce(lpart[:, :], lprod[:, :, :], AX.X, ALU.add).then_inc(lpart_ready, 1)

            choose(1)
            dve.sem_inc(unit_out, 1)

            def step(t):
                n = dve.snap(t + 1)
                cell(n, dve.snap(t * 2 + 2))
                logit_parts(n)
                choose(dve.snap(t + 2))
                return n

            with dve.Fori(0, CHUNKS) as c:
                with dve.Fori(0, SUB) as u:
                    n = step(dve.snap(c * SUB + u))
                    column = dve.snap((c % SG) * SUB + u)
                    dve.wait_ge(gx_stored, dve.snap(c * 16 + 16 * (SG + 1)))
                    dve.wait_ge(unit_mm, n)
                    dve.tensor_scalar(gx_next[:, bass.ds(c % 2, 1), :, bass.ds(u, 1)].rearrange("p a t c -> p (a t c)"), unit_ps,
                                      gscale[:, bass.ds(column, 1)], biases[:, bass.ds(column, 1)],
                                      ALU.mult, ALU.add).then_inc(unit_out, 1)
            with dve.Fori(CHUNKS * SUB, N - 1) as t:
                step(t)
            cell(N, 2 * N)
            for t in range(RT):
                b = t % 2
                rows = P if t < RT - 1 else LAST
                if t >= 2:
                    dve.wait_ge(out_done[b], 16 * (t // 2))
                dve.wait_ge(x1_back[b], 16 * (t // 2 + 1))
                dve.wait_ge(out_mm, t + 1)
                x1_v = x1_t[0:rows, b, :].rearrange("p (j s q) -> p s j q", j=4, s=SUB)
                out_v = out_t[0:rows, b, :].rearrange("p (j s q) -> p s j q", j=4, s=SUB)
                for s in range(SUB):
                    dve.scalar_tensor_tensor(out=out_v[:, s, :, :],
                                             in0=ps[0:rows, 2 + b, s * P:(s + 1) * P].rearrange("p (j q) -> p j q", j=4),
                                             scalar=float(2.0 ** -(B + 1)), in1=x1_v[:, s, :, :],
                                             op0=ALU.mult, op1=ALU.add).then_inc(out_sum, 1)

        @block.tensor
        def _(pe):
            pe.wait_ge(consts, 1)
            pe.wait_ge(small_in, 16 * 5)
            nc.tensor.matmul(ps[:, 7, 0:3 + S], ones[0:1, :], scal[0:1, :], start=True, stop=True).then_inc(scal_mm, 1)
            pe.wait_ge(masks, 4)
            pe.wait_ge(scal_mm, 2)

            def transposes(src, first, ready, want):
                for k in range(KC):
                    for q, (r0, m) in enumerate(TQ):
                        i = first + k * len(TQ) + q
                        if i >= 8:
                            pe.wait_ge(trans_out, i - 7)
                        for r in range(r0, r0 + m):
                            if k == 0:
                                pe.wait_ge(ready, r + 1)
                            last = nc.tensor.transpose(ps[:, i % 8, (r - r0) * P:(r - r0 + 1) * P],
                                                       src[:, r, k * P:(k + 1) * P], ident[:, :])
                        last.then_inc(trans_mm, 1)

            transposes(O1, 0, xn_ready, 0)
            pe.wait_ge(trans_out, NTQ)
            with pe.Fori(0, EIT) as i:
                n = pe.snap(i + 1)
                for b in range(NQ):
                    pe.wait_ge(kd_ready[b], n)
                    nc.tensor.matmul(ps[:, 2 * b, 0:P], ones[:, :], kdiag[:, b, :], start=True, stop=True).then_inc(kr_ready[b], 1)
                for b in range(NQ):
                    pe.wait_ge(same_ready[b], n)
                    nc.tensor.matmul(ps[:, 2 * b + 1, 0:1], same[:, b, :], ew[:, bass.ds(i * NQ + b, 1)],
                                     start=True, stop=True).then_inc(total_mm[b], 1)
            for q in range(NQ):
                pe.wait_ge(edge_out[q], EIT)
            for r in range(RT):
                for c, (c0, m) in enumerate(COLS):
                    if r >= 2:
                        pe.wait_ge(sim_exp, NCH * (r - 2) + c + 1)
                    for k in range(KC):
                        last = nc.tensor.matmul(ps[:, 2 + 3 * (r % 2) + c, 0:m], xT[:, k, r * P:(r + 1) * P],
                                                xT[:, k, c0:c0 + m], start=(k == 0), stop=(k == KC - 1))
                    last.then_inc(sim_mm, 1)
            pe.wait_ge(adj_ready, RT)
            for c, (c0, m) in enumerate(COLS):
                for r in range(RT):
                    last = nc.tensor.matmul(ps[:, c, 0:m], ones[:, :], Adj[:, r, c0:c0 + m], start=(r == 0), stop=(r == RT - 1))
            last.then_inc(deg_mm, 1)
            pe.wait_ge(prop_ready, 1)
            with pe.Fori(0, ITERS // 2) as i:
                for half in range(2):
                    old = O_parts[1 - half]
                    for r in range(RT):
                        pe.wait_ge(t_ready, pe.snap(i * (2 * RT) + (half * RT + r + RT - (1 if r < RT - 8 else 7))))
                        for c in range(RT):
                            if r == 0:
                                pe.wait_ge(t_low, pe.snap(i * (2 * RT) + (half * RT + c + 1)))
                            for m_part, o_part in ((0, 0), (0, 1), (1, 0)):
                                last = nc.tensor.matmul(ps[:, r % 8, :], M_parts[:, m_part, c, r * P:(r + 1) * P], old[:, o_part, c, :],
                                                        start=(c == 0 and m_part + o_part == 0), stop=(c == RT - 1 and m_part == 1))
                        last.then_inc(prop_mm, 1)
            transposes(O1, NTQ, y_ready, 0)
            pe.wait_ge(trans_out, 2 * NTQ)
            pe.sem_inc(graph_free, 1)
            for t in range(RT):
                for k in range(KC):
                    last = nc.tensor.matmul(ps[:, 0, t * S:(t + 1) * S], xT[:, k, t * P:(t + 1) * P], wselx[:, k, :],
                                            start=(k == 0), stop=(k == KC - 1))
            last.then_inc(lx_mm, 1)
            pe.wait_ge(lx_ready, 1)
            with pe.Fori(0, S) as s:
                n16 = pe.snap(s * 16 + 16)
                for g in range(G):
                    pe.wait_ge(wih_in[g], n16)
                    for u in range(SUB):
                        c = g * SUB + u
                        pe.wait_ge(proj_out, pe.snap(s * (G * SUB) + (c + 1)))
                        for k in range(KC):
                            last = nc.tensor.matmul(ps[:, c % 8, 0:TB], wih[:, g, k, u * P:(u + 1) * P],
                                                    xT[:, k, 0:TB], start=(k == 0), stop=(k == KC - 1))
                        last.then_inc(proj_mm, 1)
            for b in range(WB):
                pe.wait_ge(whh_low[b], WIT + 1)

            def products(s, n, first):
                if first:
                    pe.wait_ge(h_ready, n)
                for k in range(KC):
                    for part in range(2):
                        if first and k == 1 and part == 0:
                            pe.wait_ge(lpart_ready, n)
                            nc.tensor.matmul(logit_ps, ones[:, 0:1], lpart[:, :], start=True, stop=True).then_inc(logits_mm, 1)
                        for j in range(4):
                            nc.tensor.matmul(gate_ps[32 * j:32 * j + 17, :], hparts[:, k, :], WH[:, s * KC + k, part, j, :],
                                             start=(k == 0 and part == 0), stop=(k == KC - 1 and part == 1),
                                             tile_position=(0, 32 * j))

            def products_of(chosen, n, first):
                with pe.If_lt(chosen, 3):
                    with pe.If_lt(chosen, 2):
                        products(3, n, first)
                    with pe.Else():
                        products(2, n, first)
                with pe.Else():
                    with pe.If_lt(chosen, 4):
                        products(1, n, first)
                    with pe.Else():
                        products(0, n, first)

            guess = pe.alloc_register("guess")
            chosen = pe.alloc_register("chosen")
            column = pe.alloc_register("column")
            pe.wait_ge(rows_in, 32)
            pe.sem_inc(pick_seen, 1)

            def step(t, n):
                pe.reg_load(guess, pick_row[0:1, bass.ds(t, 1)])
                products_of(guess, n, True)
                pe.wait_ge(pick_ready, n)
                pe.sem_inc(pick_seen, 1)
                pe.reg_load(chosen, pick[0:1, 0:1])
                with pe.If_ne(chosen, guess):
                    products_of(chosen, n, False)
                nc.tensor.matmul(seal_ps, hparts[:, 0, 0:1], hparts[:, 0, 0:1], start=True, stop=True).then_inc(gates_mm, 1)

            def unit(c, u, n, w_in):
                pe.wait_ge(wih_next_in, w_in)
                pe.wait_ge(unit_out, n)
                for k in range(KC):
                    last = nc.tensor.matmul(unit_ps, wih_next[:, u, k, :], xT[:, k, bass.ds((c // SG) * TB + TB, TB)],
                                            start=(k == 0), stop=(k == KC - 1))
                last.then_inc(unit_mm, 1)

            with pe.Fori(0, CHUNKS) as c:
                with pe.Fori(0, SUB) as u:
                    t = pe.snap(c * SUB + u)
                    n = pe.snap(t + 1)
                    step(t, n)
                    w_in = pe.snap(t * 16 + 16)
                    pe.reg_mov(column, u)
                    with pe.If_lt(column, 2):
                        with pe.If_lt(column, 1):
                            unit(c, 0, n, w_in)
                        with pe.Else():
                            unit(c, 1, n, w_in)
                    with pe.Else():
                        with pe.If_lt(column, 3):
                            unit(c, 2, n, w_in)
                        with pe.Else():
                            unit(c, 3, n, w_in)
            with pe.Fori(CHUNKS * SUB, N) as t:
                step(t, pe.snap(t + 1))
                for _ in range(WARM):
                    nc.tensor.matmul(ps[:, 2, :], WH[:, 0, 0, 0, 0:P], WH[:, 0, 0, 0, :], start=True, stop=True)
            pe.wait_ge(hist_free, N + 1)
            for t in range(RT):
                rows = P if t < RT - 1 else LAST
                if t >= 2:
                    pe.wait_ge(out_sum, SUB * (t - 1))
                for s in range(SUB):
                    last = nc.tensor.transpose(ps[0:rows, 2 + t % 2, s * P:(s + 1) * P], hist[:, s, t * P:t * P + rows], ident[:, :])
                last.then_inc(out_mm, 1)


def kernel(**inputs):
    import numpy as np
    import concourse.bacc as bacc
    from concourse import mybir as mb
    from concourse.bass_utils import run_bass_kernel_spmd

    get = {k: np.asarray(val) for k, val in inputs.items()}
    P, D, S = 128, get["x"].shape[1], get["L0_ffn_W_ih"].shape[0]
    edges = get["src"].shape[0]
    main = edges // P * P
    order = [0, 1, 3, 2]

    def cut(a):
        return a[:main].reshape(P, main // P), a[main:].reshape(edges - main, 1)

    def by_unit(a):
        a = a.reshape(S, 4, 4, 4, 32)[::-1, order]
        return a.transpose(2, 4, 0, 1, 3).reshape(P, S * 16)

    whh = get["L0_ffn_W_hh"].reshape(S, 4, 4, P, 4, 4, 32)[:, order]
    whh = whh.transpose(4, 6, 0, 5, 2, 1, 3).reshape(P, S * 4 * 4 * D)
    wih = get["L0_ffn_W_ih"].reshape(S, 4, 4, 4, 32, 4, P)[::-1, order]
    wih = wih.transpose(6, 0, 1, 5, 3, 2, 4).reshape(P, S, 4, 4 * D)
    wsel = get["L0_ffn_W_sel"]
    wsel_h = wsel[:, 0:D].reshape(S, 4, 4, 32).transpose(1, 3, 0, 2).reshape(P, S, 4)
    wsel_c = wsel[:, D:2 * D].reshape(S, 4, 4, 32).transpose(1, 3, 0, 2).reshape(P, S, 4)
    src_main, src_tail = cut(get["src"])
    dst_main, dst_tail = cut(get["dst"])
    ew_main, ew_tail = cut(get["edge_weight"])
    arrays = {
        "x": get["x"],
        "src_main": src_main, "src_tail": src_tail,
        "dst_main": dst_main, "dst_tail": dst_tail,
        "ew_main": ew_main, "ew_tail": ew_tail,
        "scalars": np.concatenate([get["L0_gnn_alpha"], get["L0_gnn_beta"], get["L0_gnn_sigma"], get["L0_ffn_b_sel"]]).reshape(1, 3 + S),
        "w_ih": wih, "w_hh": whh,
        "b_ih": by_unit(get["L0_ffn_b_ih"]), "b_hh": by_unit(get["L0_ffn_b_hh"]),
        "w_sel_state": np.concatenate([wsel_c, wsel_h], axis=2),
        "w_sel_x": wsel[:, 2 * D:3 * D].reshape(S, 4, P).transpose(2, 1, 0),
    }
    nc = bacc.Bacc("TRN2", target_bir_lowering=False, num_devices=1)
    given, args = {}, []
    for name, a in arrays.items():
        a = np.ascontiguousarray(a)
        given[f"in_{name}"] = a
        args.append(nc.dram_tensor(f"in_{name}", a.shape, mb.dt.from_np(a.dtype), kind="ExternalInput").ap())
    out = nc.dram_tensor("out_rows", get["x"].shape, mb.dt.from_np(get["x"].dtype), kind="ExternalOutput").ap()
    gnn_then_selected_lstm(nc, *args, out)
    r = run_bass_kernel_spmd(nc, [given], core_ids=[0])
    return r.results[0]["out_rows"]
```
